# Optimizing a Trainium2 kernel written in Bass

```python
import numpy as np
import jax
import jax.numpy as jnp

def _softmax(x, axis=-1):
    return jax.nn.softmax(x, axis=axis)

def _gelu(x):
    return jax.nn.gelu(x, approximate=True)

def _silu(x):
    return jax.nn.silu(x)

def _sigmoid(x):
    return jax.nn.sigmoid(x)

def _layernorm(x, axis=-1, eps=1e-05):
    m = jnp.mean(x, axis=axis, keepdims=True)
    v = jnp.var(x, axis=axis, keepdims=True)
    return (x - m) / jnp.sqrt(v + eps)

def _scatter_add(tgt, idx, src, axis=0):
    return tgt.at[idx].add(src)

def _segment_sum(src, seg, n):
    return jax.ops.segment_sum(src, seg, n)
kernel_name = 'mk_prb_d1_jaxref_r8_bd8a87'

def setup_inputs(seed: int=0):
    np.random.seed(seed)
    _w = jnp.asarray

    def _L0_attn_setup():
        import jax, jax.numpy as jnp
        import numpy as np
        N_EMBD = 128
        BLOCK_SIZE = 256
        B = 8
        LN_EPS = 1e-05

        def _mlp(x, W1, b1, W2, b2):
            h = jax.nn.gelu(x @ W1 + b1, approximate=False)
            return h @ W2 + b2
        key = jax.random.key(seed)
        ks = jax.random.split(key, 14)
        C = N_EMBD
        std = 0.02
        d = {'x': jax.random.normal(ks[0], (B, BLOCK_SIZE, C), dtype=jnp.float32)}
        names = ['q', 'k', 'v']
        i = 1
        for n in names:
            d[f'W1{n}'] = jax.random.normal(ks[i], (C, C), dtype=jnp.float32) * std
            i += 1
            d[f'b1{n}'] = jnp.zeros((C,), dtype=jnp.float32)
            d[f'W2{n}'] = jax.random.normal(ks[i], (C, C), dtype=jnp.float32) * std
            i += 1
            d[f'b2{n}'] = jnp.zeros((C,), dtype=jnp.float32)
        d['ln_w'] = jnp.ones((C,), dtype=jnp.float32)
        d['ln_b'] = jnp.zeros((C,), dtype=jnp.float32)
        return d
    _L0_attn_in = _L0_attn_setup()

    def _L0_ffn_setup():
        import jax, jax.numpy as jnp
        import numpy as np
        D = 128
        E = 12
        HS = 2 * D
        HR = 3 * D
        TAU = 1.5

        def _geglu(h):
            a, g = jnp.split(h, 2, axis=-1)
            return a * jax.nn.gelu(g, approximate=False)
        key = jax.random.key(seed)
        ks = jax.random.split(key, 12)

        def xavier(k, shape):
            fan_in, fan_out = (shape[-2], shape[-1])
            lim = jnp.sqrt(6.0 / (fan_in + fan_out))
            return jax.random.uniform(k, shape, jnp.float32, -lim, lim)
        x = jax.random.normal(ks[0], (2, 128, D), jnp.float32)
        Ws1 = xavier(ks[1], (D, 2 * HS))
        bs1 = jnp.zeros((2 * HS,), jnp.float32)
        Ws2 = xavier(ks[2], (HS, D))
        bs2 = jnp.zeros((D,), jnp.float32)
        We1 = xavier(ks[3], (E, D, 2 * HR))
        be1 = jnp.zeros((E, 2 * HR), jnp.float32)
        We2 = xavier(ks[4], (E, HR, D))
        be2 = jnp.zeros((E, D), jnp.float32)
        Wr = xavier(ks[5], (D, E))
        br = jnp.zeros((E,), jnp.float32)
        return {'x': x, 'Ws1': Ws1, 'bs1': bs1, 'Ws2': Ws2, 'bs2': bs2, 'We1': We1, 'be1': be1, 'We2': We2, 'be2': be2, 'Wr': Wr, 'br': br}
    _L0_ffn_in = _L0_ffn_setup()
    _d = {'L0_attn_x': _L0_attn_in['x'], 'L0_attn_W1q': _L0_attn_in['W1q'], 'L0_attn_b1q': _L0_attn_in['b1q'], 'L0_attn_W2q': _L0_attn_in['W2q'], 'L0_attn_b2q': _L0_attn_in['b2q'], 'L0_attn_W1k': _L0_attn_in['W1k'], 'L0_attn_b1k': _L0_attn_in['b1k'], 'L0_attn_W2k': _L0_attn_in['W2k'], 'L0_attn_b2k': _L0_attn_in['b2k'], 'L0_attn_W1v': _L0_attn_in['W1v'], 'L0_attn_b1v': _L0_attn_in['b1v'], 'L0_attn_W2v': _L0_attn_in['W2v'], 'L0_attn_b2v': _L0_attn_in['b2v'], 'L0_attn_ln_w': _L0_attn_in['ln_w'], 'L0_attn_ln_b': _L0_attn_in['ln_b'], 'L0_ffn_Ws1': _L0_ffn_in['Ws1'], 'L0_ffn_bs1': _L0_ffn_in['bs1'], 'L0_ffn_Ws2': _L0_ffn_in['Ws2'], 'L0_ffn_bs2': _L0_ffn_in['bs2'], 'L0_ffn_We1': _L0_ffn_in['We1'], 'L0_ffn_be1': _L0_ffn_in['be1'], 'L0_ffn_We2': _L0_ffn_in['We2'], 'L0_ffn_be2': _L0_ffn_in['be2'], 'L0_ffn_Wr': _L0_ffn_in['Wr'], 'L0_ffn_br': _L0_ffn_in['br']}
    _x0 = _d['L0_attn_x']
    _d['L0_attn_x'] = jax.random.normal(jax.random.fold_in(jax.random.key(seed), 1), (8, 512, 128), dtype=_x0.dtype)
    del _x0
    return _d

def reference(L0_attn_x, L0_attn_W1q, L0_attn_b1q, L0_attn_W2q, L0_attn_b2q, L0_attn_W1k, L0_attn_b1k, L0_attn_W2k, L0_attn_b2k, L0_attn_W1v, L0_attn_b1v, L0_attn_W2v, L0_attn_b2v, L0_attn_ln_w, L0_attn_ln_b, L0_ffn_Ws1, L0_ffn_bs1, L0_ffn_Ws2, L0_ffn_bs2, L0_ffn_We1, L0_ffn_be1, L0_ffn_We2, L0_ffn_be2, L0_ffn_Wr, L0_ffn_br):

    def _L0_attn_ref(x, W1q, b1q, W2q, b2q, W1k, b1k, W2k, b2k, W1v, b1v, W2v, b2v, ln_w, ln_b):
        import jax, jax.numpy as jnp
        import numpy as np
        N_EMBD = 128
        BLOCK_SIZE = 256
        B = 8
        LN_EPS = 1e-05

        def _mlp(x, W1, b1, W2, b2):
            h = jax.nn.gelu(x @ W1 + b1, approximate=False)
            return h @ W2 + b2
        Bsz, T, C = x.shape
        q = _mlp(x, W1q, b1q, W2q, b2q)
        k = _mlp(x, W1k, b1k, W2k, b2k)
        v = _mlp(x, W1v, b1v, W2v, b2v)
        scale = np.sqrt(N_EMBD * BLOCK_SIZE).astype(np.float32)
        scores = jnp.einsum('bid,bjd->bij', q, k) / scale
        mask = jnp.tril(jnp.ones((T, T), dtype=scores.dtype))
        scores = scores * mask
        out = jnp.einsum('bij,bjd->bid', scores, v)
        mu = jnp.mean(out, axis=-1, keepdims=True)
        var = jnp.mean(jnp.square(out - mu), axis=-1, keepdims=True)
        out = (out - mu) * jax.lax.rsqrt(var + LN_EPS) * ln_w + ln_b
        return out

    def _L0_ffn_ref(x, Ws1, bs1, Ws2, bs2, We1, be1, We2, be2, Wr, br):
        import jax, jax.numpy as jnp
        import numpy as np
        D = 128
        E = 12
        HS = 2 * D
        HR = 3 * D
        TAU = 1.5

        def _geglu(h):
            a, g = jnp.split(h, 2, axis=-1)
            return a * jax.nn.gelu(g, approximate=False)
        B, T, Dm = x.shape
        xf = x.reshape(-1, Dm)
        ys = _geglu(xf @ Ws1 + bs1) @ Ws2 + bs2
        logits = (xf @ Wr + br) / TAU
        top_val, top_idx = jax.lax.top_k(logits, 2)
        top_w = jax.nn.softmax(top_val, axis=-1)
        onehot = jax.nn.one_hot(top_idx, E, dtype=x.dtype)
        w = jnp.einsum('nke,nk->ne', onehot, top_w)
        h = jnp.einsum('nd,edh->enh', xf, We1) + be1[:, None, :]
        act = _geglu(h)
        yE = jnp.einsum('enh,ehd->end', act, We2) + be2[:, None, :]
        yr = jnp.einsum('end,ne->nd', yE, w)
        return (ys + yr).reshape(B, T, Dm)
    x = L0_attn_x
    xn = _layernorm(x, axis=-1)
    x = x + _L0_attn_ref(xn, L0_attn_W1q, L0_attn_b1q, L0_attn_W2q, L0_attn_b2q, L0_attn_W1k, L0_attn_b1k, L0_attn_W2k, L0_attn_b2k, L0_attn_W1v, L0_attn_b1v, L0_attn_W2v, L0_attn_b2v, L0_attn_ln_w, L0_attn_ln_b) + _L0_ffn_ref(xn, L0_ffn_Ws1, L0_ffn_bs1, L0_ffn_Ws2, L0_ffn_bs2, L0_ffn_We1, L0_ffn_be1, L0_ffn_We2, L0_ffn_be2, L0_ffn_Wr, L0_ffn_br)
    return x

_drawn_inputs = setup_inputs


def setup_inputs(seed=0):
    import zlib

    import numpy as np

    out = dict(_drawn_inputs(seed))
    spreads = {'L0_attn_b1q': (0.0, 0.1),
     'L0_attn_b2q': (0.0, 0.1),
     'L0_attn_b1k': (0.0, 0.1),
     'L0_attn_b2k': (0.0, 0.1),
     'L0_attn_b1v': (0.0, 0.1),
     'L0_attn_b2v': (0.0, 0.1),
     'L0_attn_ln_w': (1.0, 0.2),
     'L0_attn_ln_b': (0.0, 0.1),
     'L0_ffn_bs1': (0.0, 0.1),
     'L0_ffn_bs2': (0.0, 0.1),
     'L0_ffn_be1': (0.0, 0.272),
     'L0_ffn_be2': (0.0, 0.1),
     'L0_ffn_br': (0.0, 0.1)}
    factors = {'L0_attn_W1v': 2.769}
    for name, (base, spread) in spreads.items():
        noise = np.random.default_rng([zlib.crc32(name.encode()), seed]).standard_normal(out[name].shape)
        drawn = base * np.exp(spread * noise) if base else spread * noise
        out[name] = jnp.asarray(drawn.astype(out[name].dtype))
    for name, factor in factors.items():
        out[name] = (out[name] * factor).astype(out[name].dtype)
    return out
```

```python
import concourse.bass as bass
from concourse import mybir
from contextlib import ExitStack

P = 128
BATCH, SEQ, D = 8, 512, 128
TOKENS = BATCH * SEQ
TPB = SEQ // P
TILES = TOKENS // P
E, TOP = 12, 2
HS, HR = 2 * D, 3 * D
CS, CR = HS // P, HR // P
SLOTS = 256
SUB = SLOTS // P
EXPERT_TILES = (TOP * TOKENS + E * (SLOTS - 1)) // SLOTS
ALL_SLOTS = EXPERT_TILES * SLOTS
EPS = 1e-5
INV_SCALE = 1.0 / float(128 * 256) ** 0.5
INV_TAU = 1.0 / 1.5
MASKED = -3.0e38

C_ID = 0
C_MASK = C_ID + P
C_BEFORE = C_MASK + SEQ
C_REV = C_BEFORE + P
C_TILE = C_REV + E * TILES
C_ALL = C_TILE + EXPERT_TILES * E

B_1 = 0
B_2 = 3
B_S1 = 5
B_E1 = B_S1 + 2 * CS
B_ALL = B_E1 + E * 2 * CR

R_BR = 0
R_B2V = R_BR + E
R_LNW = R_B2V + D
R_LNB = R_LNW + D
R_BS2 = R_LNB + D
R_BE2 = R_BS2 + D
R_ALL = R_BE2 + E * D


def block_kernel(nc, x, w1, w2, ws1, ws2, we1, we2, wr, consts, bias_cols, bias_rows, out):
    fp32, bf16, i32, u32 = mybir.dt.float32, mybir.dt.bfloat16, mybir.dt.int32, mybir.dt.uint32
    ALU, ACT, AX = mybir.AluOpType, mybir.ActivationFunctionType, mybir.AxisListType
    ds = bass.ds

    x_tiled = x.rearrange("b (t p) d -> p (b t) d", p=P)
    out_tiled = out.rearrange("b (t p) d -> p (b t) d", p=P)
    slot_x = nc.dram_tensor("slot_x", [ALL_SLOTS, D], fp32, kind="Internal").ap()
    slot_y = nc.dram_tensor("slot_y", [ALL_SLOTS, D], fp32, kind="Internal").ap()
    slot_x_flat = slot_x.rearrange("(p r) d -> p (r d)", p=P)
    slot_x_tiled = slot_x.rearrange("(t p) d -> p t d", p=P)
    slot_y_tiled = slot_y.rearrange("(t p) d -> p t d", p=P)
    we1_rows = we1.rearrange("e d h -> (e d) h")
    we2_rows = we2.rearrange("e (c p) d -> p (e c) d", p=P)

    ctx = ExitStack()
    with ctx:
        def sb(name, shape, dt=fp32):
            return ctx.enter_context(nc.sbuf_tensor(name, shape, dt))

        def sem(name):
            return ctx.enter_context(nc.semaphore(name))

        x_all = sb("x_all", [P, TILES, D])
        xn_all = sb("xn_all", [P, TILES, D])
        xnT_all = sb("xnT_all", [P, TOKENS])
        qT_all = sb("qT_all", [P, TOKENS])
        kT_all = sb("kT_all", [P, TOKENS])
        v_all = sb("v_all", [P, TILES, D])
        acc = sb("acc", [P, TILES, D])
        y0_all, y1_all = xn_all, x_all
        o_all = xnT_all[:, :].rearrange("p (t d) -> p t d", d=D)
        zeros = acc[:, :, :].rearrange("p t d -> p (t d)")

        w1_sb = sb("w1_sb", [P, 3, D])
        w2_sb = sb("w2_sb", [P, 3, D])
        ws1_sb = sb("ws1_sb", [P, 2 * HS])
        ws2_sb = sb("ws2_sb", [P, CS, D])
        wr_sb = sb("wr_sb", [P, E])
        cst = sb("cst", [P, C_ALL])
        bcol = sb("bcol", [P, B_ALL])
        brow = sb("brow", [P, R_ALL])
        ident = cst[:, C_ID:C_ID + P]
        mask = cst[:, C_MASK:C_MASK + SEQ]
        rev = cst[:, C_REV:C_REV + E * TILES]
        tile_no = cst[:, C_TILE:C_TILE + EXPERT_TILES * E]
        before_bf = sb("before_bf", [P, P], bf16)
        ones_bf = sb("ones_bf", [P, P], bf16)
        qbias = sb("qbias", [P, 1])
        lnb_bs2 = sb("lnb_bs2", [P, D])
        half_neg = sb("half_neg", [P, TILES])

        eps_sb = sb("eps_sb", [P, TPB])

        stats = sb("stats", [P, 2, TPB, 6])
        mv = sb("mv", [P, 2, TPB, 2])
        rstd = sb("rstd", [P, 2, TPB])
        vpe = sb("vpe", [P, 2, TPB])
        xn_st = sb("xn_st", [P, 2, TPB, D])
        xnT_st = sb("xnT_st", [P, 2, SEQ])

        ET = E * TILES
        lg = sb("lg", [P, ET])
        best = sb("best", [P, TOP, TILES])
        first = sb("first", [P, TILES])
        hit = sb("hit", [P, ET])
        lg2 = sb("lg2", [P, ET])
        choice = sb("choice", [P, TOP, ET])
        taken = sb("taken", [P, ET], bf16)
        ones_et = sb("ones_et", [P, ET])
        total = sb("total", [P, ET])
        cum = sb("cum", [P, ET])
        pos = sb("pos", [P, ET])
        picked = sb("picked", [P, ET])
        cnt_f = sb("cnt_f", [P, E])
        cnt_i = sb("cnt_i", [P, E], i32)
        tiles_i = sb("tiles_i", [P, E], i32)
        tiles_f = sb("tiles_f", [P, E])
        tile_end = sb("tile_end", [P, E])
        run_off = sb("run_off", [P, E])
        slot_f = sb("slot_f", [P, TOP, TILES])
        slot = sb("slot", [P, TOP, TILES], u32)
        ended = sb("ended", [P, EXPERT_TILES * E])
        owner_f = sb("owner_f", [P, EXPERT_TILES])
        owner = sb("owner", [P, EXPERT_TILES], i32)
        gap = sb("gap", [P, TILES])
        ratio = sb("ratio", [P, TILES])
        denom = sb("denom", [P, TILES])
        weight = sb("weight", [P, TOP, TILES])

        h_sb = sb("h_sb", [P, 2, SEQ])
        gate_sb = sb("gate_sb", [P, 2, SEQ])
        sT = sb("sT", [P, 2, TPB, SEQ])
        act_sb = sT[:, 0, :, :].rearrange("p (u c) s -> p u c s", u=2)
        we1_sb = sb("we1_sb", [P, 2, 2 * HR])
        we2_sb = sb("we2_sb", [P, 2, CR, D])
        eb1 = sb("eb1", [P, 2, 2 * CR])
        eb2 = sb("eb2", [P, 2, D])
        xs_sb = xn_st[:, :, 0:SUB, :]
        xsT_sb = xnT_st[:, :, 0:SLOTS]
        egate = gate_sb[:, :, 0:SLOTS]
        eact = sT[:, 1, 0:CR, :].rearrange("p c (u s) -> p u c s", u=2)
        ys_sb = sb("ys_sb", [P, 2, SUB, D])
        kT_st = h_sb
        o_stats = stats
        o_mv = mv
        mv_all = sb("mv_all", [P, TILES, 2])
        o_vpe = sb("o_vpe", [P, TILES])
        o_rstd = sb("o_rstd", [P, TILES])

        bank = [ctx.enter_context(nc.psum_tensor(f"bank{i}", [P, 512], fp32)) for i in range(8)]

        const_in, w_in = sem("const_in"), sem("w_in")
        x_in = [sem("x_in0"), sem("x_in1")]
        prep = sem("prep")
        wait_holder = sem("wait_holder")
        a_bn, a_mv, a_rstd, a_xn = sem("a_bn"), sem("a_mv"), sem("a_rstd"), sem("a_xn")
        a_pool, a_vpe = sem("a_pool"), sem("a_vpe")
        a_tr, a_st, a_all, a_lg = sem("a_tr"), sem("a_st"), sem("a_all"), sem("a_lg")
        a_keep = sem("a_keep")
        r_step, r_mask, r_rank, r_slot, r_owner = sem("r_step"), sem("r_mask"), sem("r_rank"), sem("r_slot"), sem("r_owner")
        r_gap, r_exp = sem("r_gap"), sem("r_exp")
        zeros_set, zero_fill, scattered = sem("zeros_set"), sem("zero_fill"), sem("scattered")
        b_h, b_gelu, b_o, b_evac, b_v = sem("b_h"), sem("b_gelu"), sem("b_o"), sem("b_evac"), sem("b_v")
        d_g, d_a, d_gate, d_act, d_y, d_acc = sem("d_g"), sem("d_a"), sem("d_gate"), sem("d_act"), sem("d_y"), sem("d_acc")
        d_step = sem("d_step")
        e_x = [sem("e_x0"), sem("e_x1")]
        e_w = [sem("e_w0"), sem("e_w1")]
        e_st = [sem("e_st0"), sem("e_st1")]
        e_bias, e_tr, e_xT, e_g, e_a = sem("e_bias"), sem("e_tr"), sem("e_xT"), sem("e_g"), sem("e_a")
        e_gate, e_act, e_y, e_yev = sem("e_gate"), sem("e_act"), sem("e_y"), sem("e_yev")
        c_k, c_s, c_mask, c_o, c_oev, c_bn, c_mv, c_keep = (sem("c_k"), sem("c_s"), sem("c_mask"), sem("c_o"),
                                                           sem("c_oev"), sem("c_bn"), sem("c_mv"), sem("c_keep"))
        c_vpe, c_rstd = sem("c_vpe"), sem("c_rstd")
        gathered = [sem("gathered0"), sem("gathered1")]
        f_norm, f_w, f_res, f_y0, f_done = sem("f_norm"), sem("f_w"), sem("f_res"), sem("f_y0"), sem("f_done")
        stored = sem("stored")

        RING = 2
        B_ITEMS = 3 * BATCH
        D_ITEMS = CS * BATCH
        PAIRS = BATCH // 2
        E_PAIRS = EXPERT_TILES // 2

        block = ctx.enter_context(nc.Block())

        @block.sync
        def _(sp):
            sp.sem_inc(e_st[0], 16)
            sp.sem_inc(e_st[1], 16)
            sp.dma_start(cst[:, :], consts).then_inc(const_in, 16)
            with sp.Fori(0, PAIRS) as i:
                for u in range(2):
                    sp.wait_ge(x_in[u], 16 * i + 16)
                    sp.dma_start(x_all[:, ds((2 * i + u) * TPB, TPB), :],
                                 x_tiled[:, ds((2 * i + u) * TPB, TPB), :]).then_inc(x_in[u], 16)
            for dst, src in ((wr_sb[:, :], wr), (brow[:, :], bias_rows), (bcol[:, :], bias_cols)):
                sp.dma_start(dst, src).then_inc(const_in, 16)
            for n in range(3):
                sp.dma_start(w1_sb[:, n, :], w1[n]).then_inc(w_in, 16)
                sp.dma_start(w2_sb[:, n, :], w2[n]).then_inc(w_in, 16)
            sp.dma_start(ws1_sb[:, :], ws1).then_inc(w_in, 16)
            sp.dma_start(ws2_sb[:, :, :], ws2.rearrange("(c p) d -> p c d", p=P)).then_inc(w_in, 16)
            sp.wait_ge(zeros_set, 1)
            width = ALL_SLOTS
            for f in range(0, width, TOKENS):
                n = min(TOKENS, width - f)
                sp.dma_start(slot_x_flat[:, f:f + n], zeros[:, 0:n]).then_inc(zero_fill, 16)

            def load(j, u, done):
                sp.wait_ge(e_y, j + 1)
                e = sp.value_load(owner[0:1, ds(j, 1)], min_val=0, max_val=E - 1)
                sp.dma_start(we1_sb[:, u, :], we1_rows[ds(e * D, D), :]).then_inc(e_w[u], 16)
                sp.dma_start(we2_sb[:, u, :, :], we2_rows[:, ds(e * CR, CR), :]).then_inc(e_w[u], 16)
                sp.wait_ge(e_tr, j + 1)
                sp.dma_start(xs_sb[:, u, :, :], slot_x_tiled[:, ds(j * SUB, SUB), :]).then_inc(e_x[u], 16)

            def store(j, u):
                sp.wait_ge(e_yev, j + 1 + RING)
                sp.dma_start(slot_y_tiled[:, ds(j * SUB, SUB), :], ys_sb[:, u, :, :]).then_inc(e_st[u], 16)

            sp.wait_ge(r_owner, 1)
            sp.wait_ge(scattered, 16 * TOP * TILES)
            load(0, 0, None)
            load(1, 1, None)
            with sp.Fori(0, E_PAIRS - 1) as i:
                for u in range(2):
                    store(2 * i + u, u)
                    load(2 * i + u + 2, u, None)
            store(EXPERT_TILES - 3, 0)
            load(EXPERT_TILES - 1, 0, None)
            store(EXPERT_TILES - 2, 1)
            store(EXPERT_TILES - 1, 0)

            with sp.Fori(0, BATCH) as b:
                sp.wait_ge(f_done, b + 1)
                sp.dma_start(out_tiled[:, ds(b * TPB, TPB), :], acc[:, ds(b * TPB, TPB), :]).then_inc(stored, 16)
            sp.wait_ge(stored, 16 * BATCH)

        @block.gpsimd
        def _(pool):
            pool.sem_inc(a_keep, RING)
            pool.sem_inc(x_in[0], 16)
            pool.sem_inc(x_in[1], 16)
            nc.gpsimd.memset(half_neg[:, :], -0.5).then_inc(prep, 1)
            nc.gpsimd.memset(eps_sb[:, :], EPS).then_inc(prep, 1)
            nc.gpsimd.memset(ones_bf[:, :], 1.0).then_inc(prep, 1)
            nc.gpsimd.memset(ones_et[:, :], 1.0).then_inc(prep, 1)
            nc.gpsimd.memset(zeros, 0.0).then_inc(zeros_set, 1)
            pool.wait_ge(prep, 4)
            with pool.Fori(0, PAIRS) as i:
                for u in range(2):
                    pool.wait_ge(a_mv, 2 * i + u + 1)
                    pool.wait_ge(a_xn, 2 * i + u + 1)
                    nc.gpsimd.tensor_tensor(vpe[:, u, :], mv[:, u, :, 1], eps_sb[:, :], ALU.add).then_inc(a_vpe, 1)
                    pool.wait_ge(a_vpe, 2 * i + u + 1)
                    nc.gpsimd.tensor_tensor(rstd[:, u, :], vpe[:, u, :], half_neg[:, 0:TPB], ALU.pow).then_inc(a_rstd, 1)
                for u in range(2):
                    pool.wait_ge(a_xn, 2 * i + u + 1 + RING)
                    nc.gpsimd.tensor_copy(xn_all[:, ds((2 * i + u) * TPB, TPB), :], xn_st[:, u, :, :]).then_inc(a_keep, 1)
            pool.wait_ge(a_keep, BATCH + RING)
            pool.wait_ge(zero_fill, 16 * -(-ALL_SLOTS // TOKENS))
            pool.wait_ge(r_slot, 1)
            for t in range(TILES):
                for k in range(TOP):
                    nc.gpsimd.indirect_dma_start(slot_x, bass.IndirectOffsetOnAxis(ap=slot[:, k, t:t + 1], axis=0),
                                                 xn_all[:, t, :], None).then_inc(scattered, 16)

            def expert_bias(j, u):
                pool.wait_ge(e_yev, j + 1)
                e = pool.value_load(owner[0:1, ds(j, 1)], min_val=0, max_val=E - 1)
                nc.gpsimd.tensor_copy(eb1[:, u, :], bcol[:, ds(B_E1 + e * 2 * CR, 2 * CR)]).then_inc(e_bias, 1)
                nc.gpsimd.tensor_copy(eb2[:, u, :], brow[:, ds(R_BE2 + e * D, D)]).then_inc(e_bias, 1)

            pool.wait_ge(r_owner, 1)
            with pool.Fori(0, E_PAIRS) as i:
                for u in range(2):
                    expert_bias(2 * i + u, u)
            expert_bias(EXPERT_TILES - 1, 0)
            pool.wait_ge(scattered, 16 * TOP * TILES)
            pool.wait_ge(e_st[0], 16 * (EXPERT_TILES - E_PAIRS) + 16)
            pool.wait_ge(e_st[1], 16 * E_PAIRS + 16)
            for b in range(BATCH):
                if b >= 2:
                    pool.wait_ge(gathered[b % 2], 16 * TOP * TPB * (b // 2))
                for t in range(b * TPB, (b + 1) * TPB):
                    for k, y in enumerate((y0_all, y1_all)):
                        nc.gpsimd.indirect_dma_start(y[:, t, :], None, slot_y,
                                                     bass.IndirectOffsetOnAxis(ap=slot[:, k, t:t + 1], axis=0)
                                                     ).then_inc(gathered[b % 2], 16)
                if b == BATCH // 2 - 1:
                    pool.wait_ge(c_keep, BATCH)
                    nc.gpsimd.tensor_scalar(o_vpe[:, :], mv_all[:, :, 1], EPS, None, ALU.add).then_inc(c_vpe, 1)
                    pool.wait_ge(c_vpe, 1)
                    nc.gpsimd.tensor_tensor(o_rstd[:, :], o_vpe[:, :], half_neg[:, :], ALU.pow).then_inc(c_rstd, 1)

        @block.scalar
        def _(act):
            for s in (a_all, a_st, b_gelu, b_evac, d_gate, e_gate, e_xT, c_oev):
                act.sem_inc(s, RING)
            act.wait_ge(const_in, 64)
            with act.Fori(0, PAIRS) as i:
                for u in range(2):
                    b = 2 * i + u
                    act.wait_ge(a_tr, b + 1 + RING)
                    act.wait_ge(a_lg, b + 1)
                    nc.scalar.activation(xnT_st[:, u, :], bank[4 + u][:, :], ACT.Copy).then_inc(a_st, 1)
                    nc.scalar.activation(xnT_all[:, ds(b * SEQ, SEQ)], bank[4 + u][:, :], ACT.Copy).then_inc(a_all, 1)
            act.wait_ge(w_in, 16 * 8)
            nc.scalar.mul(qbias[:, :], bcol[:, B_2:B_2 + 1], INV_SCALE).then_inc(prep, 1)
            act.wait_ge(prep, 7)

            def gelu(m, n, h):
                act.wait_ge(b_h, m + 1)
                act.wait_ge(b_o, m + 1)
                nc.scalar.activation(h_sb[:, h, :], bank[h][:, :], ACT.Gelu, bias=bcol[:, B_1 + n:B_1 + n + 1]).then_inc(b_gelu, 1)

            def evac(m, b, n, h):
                act.wait_ge(b_o, m + 1 + RING)
                if n == 0:
                    nc.scalar.activation(qT_all[:, ds(b * SEQ, SEQ)], bank[2 + h][:, :], ACT.Identity,
                                         bias=qbias[:, :], scale=INV_SCALE).then_inc(b_evac, 1)
                elif n == 1:
                    nc.scalar.activation(kT_all[:, ds(b * SEQ, SEQ)], bank[2 + h][:, :], ACT.Identity,
                                         bias=bcol[:, B_2 + 1:B_2 + 2]).then_inc(b_evac, 1)
                else:
                    nc.scalar.activation(v_all[:, ds(b * TPB, TPB), :],
                                         bank[2 + h][:, :].rearrange("p (t d) -> p t d", d=D), ACT.Copy).then_inc(b_evac, 1)

            def qkv_pair(i):
                for k in range(6):
                    gelu(6 * i + k, k % 3, k % 2)
                    if k:
                        evac(6 * i + k - 1, 2 * i + (k - 1) // 3, (k - 1) % 3, (k - 1) % 2)
                evac(6 * i + 5, 2 * i + 1, 2, 1)

            qkv_pair(0)
            with act.Fori(1, PAIRS) as i:
                qkv_pair(i)

            with act.Fori(0, PAIRS) as i:
                for k in range(2 * CS):
                    m = 2 * CS * i + k
                    act.wait_ge(d_g, m + 1)
                    act.wait_ge(d_act, m + 1)
                    c = k % CS
                    nc.scalar.activation(gate_sb[:, k % 2, :], bank[4 + k % 2][:, :], ACT.Gelu,
                                         bias=bcol[:, B_S1 + CS + c:B_S1 + CS + c + 1]).then_inc(d_gate, 1)

            def rows_out(j, u):
                act.wait_ge(e_tr, j + 1 + RING)
                nc.scalar.activation(xsT_sb[:, u, :], bank[2 + u][:, 0:SLOTS], ACT.Copy).then_inc(e_xT, 1)

            def expert_gates(j, u):
                act.wait_ge(e_bias, 2 * j + 2)
                for c in range(CR):
                    m = CR * j + c
                    g = (CR * u + c) % 2
                    act.wait_ge(e_g, m + 1)
                    act.wait_ge(e_act, m + 1)
                    nc.scalar.activation(egate[:, g, :], bank[4 + g][:, 0:SLOTS], ACT.Gelu,
                                         bias=eb1[:, u, CR + c:CR + c + 1]).then_inc(e_gate, 1)

            rows_out(0, 0)
            with act.Fori(0, E_PAIRS) as i:
                for u in range(2):
                    expert_gates(2 * i + u, u)
                    rows_out(2 * i + u + 1, 1 - u)
            expert_gates(EXPERT_TILES - 1, 0)

            def key_copy(b, u):
                act.wait_ge(c_o, b + 1)
                nc.scalar.activation(kT_st[:, u, :], kT_all[:, ds(b * SEQ, SEQ)], ACT.Copy).then_inc(c_k, 1)

            def rows_kept(b, u):
                act.wait_ge(c_o, b + 1 + RING)
                act.wait_ge(c_bn, b + 1)
                nc.scalar.activation(o_all[:, ds(b * TPB, TPB), :], bank[u][:, :].rearrange("p (t d) -> p t d", d=D),
                                     ACT.Copy).then_inc(c_oev, 1)

            with act.Fori(0, PAIRS) as i:
                for u in range(2):
                    key_copy(2 * i + u, u)
                for u in range(2):
                    rows_kept(2 * i + u, u)
            act.wait_ge(r_gap, 1)
            nc.scalar.activation(ratio[:, :], gap[:, :], ACT.Exp, scale=INV_TAU).then_inc(r_exp, 1)

        @block.vector
        def _(dve):
            steps = [0]

            def step(ins):
                steps[0] += 1
                ins.then_inc(r_step, 1)
                dve.wait_ge(r_step, steps[0])

            for s in (a_xn, d_act, d_acc, e_act, e_yev, c_mask):
                dve.sem_inc(s, RING)
            with dve.Fori(0, PAIRS) as i:
                for u in range(2):
                    dve.wait_ge(x_in[u], 16 * i + 32)
                    for t in range(TPB):
                        last = nc.vector.bn_stats(stats[:, u, t, :], x_all[:, ds((2 * i + u) * TPB + t, 1), :].rearrange("p a d -> p (a d)"))
                    last.then_inc(a_bn, 1)
                for u in range(2):
                    dve.wait_ge(a_bn, 2 * i + u + 1)
                    dve.sem_inc(wait_holder, 1)
                    for t in range(TPB):
                        last = nc.vector.bn_aggr(mv[:, u, t, :], stats[:, u, t, :])
                    last.then_inc(a_mv, 1)
                for u in range(2):
                    b = 2 * i + u
                    dve.wait_ge(a_rstd, b + 1)
                    dve.wait_ge(a_tr, b + 1)
                    dve.wait_ge(a_keep, b + 1)
                    for t in range(TPB):
                        last = nc.vector.tensor_scalar(xn_st[:, u, t, :],
                                                       x_all[:, ds(b * TPB + t, 1), :].rearrange("p a d -> p (a d)"),
                                                       mv[:, u, t, 0:1], rstd[:, u, t:t + 1], ALU.subtract, ALU.mult)
                    last.then_inc(a_xn, 1)
            dve.wait_ge(const_in, 64)
            nc.vector.tensor_copy(before_bf[:, :], cst[:, C_BEFORE:C_BEFORE + P]).then_inc(prep, 1)
            nc.vector.tensor_tensor(lnb_bs2[:, :], brow[:, R_LNB:R_LNB + D], brow[:, R_BS2:R_BS2 + D], ALU.add).then_inc(prep, 1)

            def et(ap):
                return ap.rearrange("p (e t) -> p e t", t=TILES)

            def te(ap):
                return ap.rearrange("p (e t) -> p t e", t=TILES)

            def over_e(ap):
                return ap.unsqueeze(1).to_broadcast([P, E, TILES])

            def over_t(ap):
                return ap.unsqueeze(2).to_broadcast([P, E, TILES])

            dve.wait_ge(a_lg, BATCH + RING)
            step(nc.vector.tensor_tensor(et(lg[:, :]), bank[6][:, 0:ET].rearrange("p (t e) -> p e t", e=E),
                                         over_t(brow[:, R_BR:R_BR + E]), ALU.add))
            src = lg
            for k in range(TOP):
                step(nc.vector.tensor_reduce(best[:, k, :], te(src[:, :]), AX.X, ALU.max))
                step(nc.vector.tensor_tensor(et(hit[:, :]), et(src[:, :]), over_e(best[:, k, :]), ALU.is_equal))
                step(nc.vector.tensor_tensor(hit[:, :], hit[:, :], rev, ALU.mult))
                step(nc.vector.tensor_reduce(first[:, :], te(hit[:, :]), AX.X, ALU.max))
                step(nc.vector.tensor_tensor(et(choice[:, k, :]), et(rev), over_e(first[:, :]), ALU.is_equal))
                if k == 0:
                    step(nc.vector.scalar_tensor_tensor(lg2[:, :], choice[:, 0, :], MASKED, lg[:, :], ALU.mult, ALU.add))
                    src = lg2
            nc.vector.tensor_tensor(taken[:, :], choice[:, 0, :], choice[:, 1, :], ALU.add).then_inc(r_mask, 1)
            nc.vector.tensor_tensor(gap[:, :], best[:, 1, :], best[:, 0, :], ALU.subtract).then_inc(r_gap, 1)
            dve.wait_ge(r_rank, 2)
            step(nc.vector.tensor_copy(total[:, :], bank[7][:, 0:ET]))
            step(nc.vector.tensor_tensor_scan(cum[:, :], ones_et[:, :], total[:, :], 0.0, ALU.mult, ALU.add))
            step(nc.vector.tensor_tensor(total[:, :], cum[:, :], total[:, :], ALU.subtract))
            step(nc.vector.tensor_tensor(cnt_f[:, :], et(cum[:, :])[:, :, TILES - 1], et(total[:, :])[:, :, 0], ALU.subtract))
            step(nc.vector.tensor_scalar(cnt_i[:, :], cnt_f[:, :], float(SLOTS - 1), None, ALU.add))
            step(nc.vector.tensor_scalar(tiles_i[:, :], cnt_i[:, :], SLOTS.bit_length() - 1, None, ALU.arith_shift_right))
            step(nc.vector.tensor_copy(tiles_f[:, :], tiles_i[:, :]))
            step(nc.vector.tensor_tensor_scan(tile_end[:, :], ones_et[:, 0:E], tiles_f[:, :], 0.0, ALU.mult, ALU.add))
            step(nc.vector.tensor_tensor(run_off[:, :], tile_end[:, :], tiles_f[:, :], ALU.subtract))
            step(nc.vector.scalar_tensor_tensor(run_off[:, :], run_off[:, :], float(SLOTS), et(total[:, :])[:, :, 0],
                                                ALU.mult, ALU.subtract))
            step(nc.vector.tensor_tensor(pos[:, :], total[:, :], bank[6][:, 0:ET], ALU.add))
            step(nc.vector.tensor_tensor(et(pos[:, :]), et(pos[:, :]), over_t(run_off[:, :]), ALU.add))
            for k in range(TOP):
                step(nc.vector.tensor_tensor(picked[:, :], choice[:, k, :], pos[:, :], ALU.mult))
                step(nc.vector.tensor_reduce(slot_f[:, k, :], te(picked[:, :]), AX.X, ALU.add))
            nc.vector.tensor_copy(slot[:, :, :], slot_f[:, :, :]).then_inc(r_slot, 1)
            step(nc.vector.tensor_tensor(ended[:, :].rearrange("p (j e) -> p j e", e=E),
                                         tile_end[:, :].unsqueeze(1).to_broadcast([P, EXPERT_TILES, E]),
                                         tile_no.rearrange("p (j e) -> p j e", e=E), ALU.is_le))
            step(nc.vector.tensor_reduce(owner_f[:, :], ended[:, :].rearrange("p (j e) -> p j e", e=E), AX.X, ALU.add))
            nc.vector.tensor_scalar(owner[:, :], owner_f[:, :], float(E - 1), None, ALU.min).then_inc(r_owner, 1)

            dve.wait_ge(zero_fill, 16 * -(-ALL_SLOTS // TOKENS))
            dve.wait_ge(prep, 7)
            y_rows = [bank[u][:, :].rearrange("p (t d) -> p t d", d=D) for u in range(2)]

            def shared_act(i, k):
                m = 2 * CS * i + k
                dve.wait_ge(d_a, m + 1)
                dve.wait_ge(d_gate, m + 1 + RING)
                if k % CS == 0:
                    dve.wait_ge(d_y, 2 * i + k // CS + 1)
                c = k % CS
                nc.vector.scalar_tensor_tensor(act_sb[:, k // CS, c, :], bank[6 + k % 2][:, :], bcol[:, B_S1 + c:B_S1 + c + 1],
                                               gate_sb[:, k % 2, :], ALU.add, ALU.mult).then_inc(d_act, 1)

            def bias_tpb(ap):
                return ap.unsqueeze(1).to_broadcast([P, TPB, D])

            def shared_out(b, u):
                at = ds(b * TPB, TPB)
                dve.wait_ge(b_evac, 3 * b + 3 + RING)
                nc.vector.tensor_tensor(v_all[:, at, :], v_all[:, at, :], bias_tpb(brow[:, R_B2V:R_B2V + D]), ALU.add).then_inc(b_v, 1)
                nc.vector.tensor_tensor(acc[:, at, :], x_all[:, at, :], bias_tpb(lnb_bs2[:, :]), ALU.add).then_inc(d_step, 1)
                dve.wait_ge(d_step, b + 1)
                dve.wait_ge(d_y, b + 1 + RING)
                nc.vector.tensor_tensor(acc[:, at, :], acc[:, at, :], y_rows[u], ALU.add).then_inc(d_acc, 1)

            with dve.Fori(0, PAIRS) as i:
                for k in range(CS + 1):
                    shared_act(i, k)
                shared_out(2 * i, 0)
                for k in range(CS + 1, 2 * CS):
                    shared_act(i, k)
                shared_out(2 * i + 1, 1)

            def expert_rows(j, u):
                for c in range(CR):
                    m = CR * j + c
                    g = (CR * u + c) % 2
                    dve.wait_ge(e_a, m + 1)
                    dve.wait_ge(e_gate, m + 1 + RING)
                    if c == 0:
                        dve.wait_ge(e_bias, 2 * j + 2)
                        dve.wait_ge(e_y, j + 1)
                    nc.vector.scalar_tensor_tensor(eact[:, u, c, :], bank[6 + g][:, 0:SLOTS], eb1[:, u, c:c + 1],
                                                   egate[:, g, :], ALU.add, ALU.mult).then_inc(e_act, 1)
                dve.wait_ge(e_y, j + 1 + RING)
                dve.wait_ge(e_st[u], 16 * (j // 2) + 16 if isinstance(j, int) else 16 * pair[0] + 16)
                for s in range(SUB):
                    last = nc.vector.tensor_tensor(ys_sb[:, u, s, :], bank[s][:, 0:D], eb2[:, u, :], ALU.add)
                last.then_inc(e_yev, 1)

            pair = [None]
            with dve.Fori(0, E_PAIRS) as i:
                pair[0] = i
                for u in range(2):
                    expert_rows(2 * i + u, u)
            expert_rows(EXPERT_TILES - 1, 0)

            def scores_out(i, k):
                m = 2 * TPB * i + k
                u, j = k // TPB, k % TPB
                w = SEQ - j * P
                dve.wait_ge(c_s, m + 1)
                nc.vector.tensor_tensor(sT[:, u, j, 0:w], bank[2 + k % 2][:, 0:w], mask[:, 0:w], ALU.mult).then_inc(c_mask, 1)

            def row_stats(b, u):
                dve.wait_ge(c_o, b + 1 + RING)
                for t in range(TPB):
                    last = nc.vector.bn_stats(o_stats[:, u, t, :], bank[u][:, t * D:(t + 1) * D])
                last.then_inc(c_bn, 1)
                dve.wait_ge(c_bn, b + 1)
                dve.sem_inc(wait_holder, 1)
                for t in range(TPB):
                    last = nc.vector.bn_aggr(o_mv[:, u, t, :], o_stats[:, u, t, :])
                last.then_inc(c_mv, 1)
                dve.wait_ge(c_mv, b + 1)
                nc.vector.tensor_copy(mv_all[:, ds(b * TPB, TPB), :], o_mv[:, u, :, :]).then_inc(c_keep, 1)

            with dve.Fori(0, PAIRS) as i:
                for k in range(TPB + 2):
                    scores_out(i, k)
                row_stats(2 * i, 0)
                for k in range(TPB + 2, 2 * TPB):
                    scores_out(i, k)
                row_stats(2 * i + 1, 1)

            dve.wait_ge(r_exp, 1)
            step(nc.vector.tensor_scalar(denom[:, :], ratio[:, :], 1.0, None, ALU.add))
            step(nc.vector.reciprocal(weight[:, 0, :], denom[:, :]))
            step(nc.vector.tensor_tensor(weight[:, 1, :], ratio[:, :], weight[:, 0, :], ALU.mult))
            dve.wait_ge(c_rstd, 1)
            dve.wait_ge(c_oev, BATCH + RING)
            rows = [[y[:, t:t + 1, :] for t in range(TPB)] for y in (y0_all, y1_all)]

            def row(ap, t):
                return ap[:, ds(t, 1), :].rearrange("p a d -> p (a d)")

            with dve.Fori(0, BATCH) as b:
                at = ds(b * TPB, TPB)
                for t in range(TPB):
                    last = nc.vector.tensor_scalar(row(o_all, b * TPB + t), row(o_all, b * TPB + t),
                                                   mv_all[:, ds(b * TPB + t, 1), 0:1].rearrange("p a b -> p (a b)"),
                                                   o_rstd[:, ds(b * TPB + t, 1)], ALU.subtract, ALU.mult)
                last.then_inc(f_norm, 1)
                dve.wait_ge(f_norm, b + 1)
                nc.vector.tensor_tensor(o_all[:, at, :], o_all[:, at, :], bias_tpb(brow[:, R_LNW:R_LNW + D]), ALU.mult).then_inc(f_w, 1)
                dve.wait_ge(f_w, b + 1)
                nc.vector.tensor_tensor(acc[:, at, :], acc[:, at, :], o_all[:, at, :], ALU.add).then_inc(f_res, 1)
            dve.wait_ge(f_res, BATCH)
            with dve.Fori(0, PAIRS) as i:
                for u in range(2):
                    b = 2 * i + u
                    dve.wait_ge(gathered[u], 16 * TOP * TPB * (i + 1))
                    for k, y in enumerate((y0_all, y1_all)):
                        for t in range(TPB):
                            a = row(acc, b * TPB + t)
                            last = nc.vector.scalar_tensor_tensor(a, row(y, b * TPB + t), weight[:, k, ds(b * TPB + t, 1)], a,
                                                                  ALU.mult, ALU.add)
                        if k == 0:
                            last.then_inc(f_y0, 1)
                            dve.wait_ge(f_y0, b + 1)
                    last.then_inc(f_done, 1)

        @block.tensor
        def _(pe):
            mm = nc.tensor.matmul
            for s in (a_tr, a_lg, b_o, d_y, e_tr, e_y, c_o):
                pe.sem_inc(s, RING)
            pe.wait_ge(const_in, 64)
            with pe.Fori(0, PAIRS) as i:
                for u in range(2):
                    b = 2 * i + u
                    pe.wait_ge(a_xn, b + 1 + RING)
                    pe.wait_ge(a_all, b + 1)
                    for t in range(TPB):
                        last = nc.tensor.transpose(bank[4 + u][:, t * P:(t + 1) * P], xn_st[:, u, t, :], ident)
                    last.then_inc(a_tr, 1)
                for u in range(2):
                    b = 2 * i + u
                    pe.wait_ge(a_st, b + 1 + RING)
                    for t in range(TPB):
                        last = mm(bank[6][:, ds((b * TPB + t) * E, E)], xnT_st[:, u, t * P:(t + 1) * P], wr_sb[:, :],
                                  start=True, stop=True)
                    last.then_inc(a_lg, 1)

            def hidden(m, b, n, h):
                pe.wait_ge(b_gelu, m + 1)
                mm(bank[h][:, :], w1_sb[:, n, :], xnT_all[:, ds(b * SEQ, SEQ)], start=True, stop=True).then_inc(b_h, 1)

            def second(m, n, h):
                pe.wait_ge(b_gelu, m + 1 + RING)
                pe.wait_ge(b_evac, m + 1)
                if n < 2:
                    mm(bank[2 + h][:, :], w2_sb[:, n, :], h_sb[:, h, :], start=True, stop=True).then_inc(b_o, 1)
                else:
                    for t in range(TPB):
                        last = mm(bank[2 + h][:, t * D:(t + 1) * D], h_sb[:, h, t * P:(t + 1) * P], w2_sb[:, n, :],
                                  start=True, stop=True)
                    last.then_inc(b_o, 1)

            def qkv_pair(i):
                for k in range(6):
                    hidden(6 * i + k, 2 * i + k // 3, k % 3, k % 2)
                    if k:
                        second(6 * i + k - 1, (k - 1) % 3, (k - 1) % 2)
                second(6 * i + 5, 2, 1)

            pe.wait_ge(w_in, 16 * 8)
            pe.wait_ge(a_all, BATCH + RING)
            qkv_pair(0)
            pe.wait_ge(r_mask, 1)
            pe.wait_ge(prep, 7)
            mm(bank[6][:, 0:ET], before_bf[:, :], taken[:, :], start=True, stop=True).then_inc(r_rank, 1)
            mm(bank[7][:, 0:ET], ones_bf[:, :], taken[:, :], start=True, stop=True).then_inc(r_rank, 1)
            with pe.Fori(1, PAIRS) as i:
                qkv_pair(i)

            def shared_up(i, k):
                m = 2 * CS * i + k
                c = k % CS
                xs = xnT_all[:, ds((2 * i + k // CS) * SEQ, SEQ)]
                pe.wait_ge(d_gate, m + 1)
                mm(bank[4 + k % 2][:, :], ws1_sb[:, HS + c * P:HS + (c + 1) * P], xs, start=True, stop=True).then_inc(d_g, 1)
                pe.wait_ge(d_act, m + 1)
                mm(bank[6 + k % 2][:, :], ws1_sb[:, c * P:(c + 1) * P], xs, start=True, stop=True).then_inc(d_a, 1)

            def shared_down(b, i, u):
                pe.wait_ge(d_act, 2 * CS * i + CS * (u + 1) + RING)
                pe.wait_ge(d_acc, b + 1)
                for t in range(TPB):
                    for c in range(CS):
                        last = mm(bank[u][:, t * D:(t + 1) * D], act_sb[:, u, c, t * P:(t + 1) * P], ws2_sb[:, c, :],
                                  start=(c == 0), stop=(c == CS - 1))
                last.then_inc(d_y, 1)

            pe.wait_ge(r_slot, 1)
            pe.wait_ge(b_evac, B_ITEMS + RING)
            with pe.Fori(0, PAIRS) as i:
                for k in range(CS + 1):
                    shared_up(i, k)
                shared_down(2 * i, i, 0)
                for k in range(CS + 1, 2 * CS):
                    shared_up(i, k)
                shared_down(2 * i + 1, i, 1)

            def slot_transposes(j, u, i):
                pe.wait_ge(e_x[u], 16 * i + 16)
                pe.wait_ge(e_xT, j + 1)
                for s in range(SUB):
                    last = nc.tensor.transpose(bank[2 + u][:, s * P:(s + 1) * P], xs_sb[:, u, s, :], ident)
                last.then_inc(e_tr, 1)

            def expert(j, u, i, last_tile=False):
                pe.wait_ge(e_w[u], 32 * i + 32)
                pe.wait_ge(e_xT, j + 1 + RING)
                for c in range(CR):
                    m = CR * j + c
                    g = (CR * u + c) % 2
                    pe.wait_ge(e_gate, m + 1)
                    mm(bank[4 + g][:, 0:SLOTS], we1_sb[:, u, HR + c * P:HR + (c + 1) * P], xsT_sb[:, u, :],
                       start=True, stop=True).then_inc(e_g, 1)
                    pe.wait_ge(e_act, m + 1)
                    mm(bank[6 + g][:, 0:SLOTS], we1_sb[:, u, c * P:(c + 1) * P], xsT_sb[:, u, :],
                       start=True, stop=True).then_inc(e_a, 1)
                pe.wait_ge(e_yev, j + 2)
                for c in range(CR):
                    pe.wait_ge(e_act, CR * j + c + 1 + RING)
                    if c == CR - 1 and not last_tile:
                        slot_transposes(j + 1, 1 - u, i + u)
                    for s in range(SUB):
                        last = mm(bank[s][:, 0:D], eact[:, u, c, s * P:(s + 1) * P], we2_sb[:, u, c, :],
                                  start=(c == 0), stop=(c == CR - 1))
                last.then_inc(e_y, 1)

            pe.wait_ge(d_acc, BATCH + RING)
            pe.wait_ge(d_act, D_ITEMS + RING)
            slot_transposes(0, 0, 0)
            with pe.Fori(0, E_PAIRS) as i:
                for u in range(2):
                    expert(2 * i + u, u, i)
            expert(EXPERT_TILES - 1, 0, E_PAIRS, True)

            def scores(i, k):
                u, j = k // TPB, k % TPB
                b = 2 * i + u
                if j == 0:
                    pe.wait_ge(c_k, b + 1)
                pe.wait_ge(c_mask, 2 * TPB * i + k + 1)
                mm(bank[2 + k % 2][:, 0:SEQ - j * P], kT_st[:, u, j * P:(j + 1) * P],
                   qT_all[:, ds(b * SEQ + j * P, SEQ - j * P)], start=True, stop=True).then_inc(c_s, 1)

            def attend(i, u):
                b = 2 * i + u
                pe.wait_ge(c_mask, 2 * TPB * i + TPB * (u + 1) + RING)
                pe.wait_ge(c_oev, b + 1)
                for t in range(TPB):
                    for j in range(t + 1):
                        last = mm(bank[u][:, t * D:(t + 1) * D], sT[:, u, j, (t - j) * P:(t - j + 1) * P],
                                  v_all[:, ds(b * TPB + j, 1), :].rearrange("p a d -> p (a d)"), start=(j == 0), stop=(j == t))
                last.then_inc(c_o, 1)

            pe.wait_ge(e_yev, EXPERT_TILES + RING)
            pe.wait_ge(e_xT, EXPERT_TILES + RING)
            pe.wait_ge(b_v, BATCH)
            with pe.Fori(0, PAIRS) as i:
                for k in range(TPB + 2):
                    scores(i, k)
                attend(i, 0)
                for k in range(TPB + 2, 2 * TPB):
                    scores(i, k)
                attend(i, 1)


def kernel(**inputs):
    import numpy as np
    import concourse.bacc as bacc
    from concourse.bass_utils import run_bass_kernel_spmd

    def a(name):
        return np.ascontiguousarray(inputs["L0_" + name])

    c = np.zeros((P, C_ALL), np.float32)
    row, col = np.arange(P)[:, None], np.arange(P)[None, :]
    c[:, C_ID:C_ID + P] = row == col
    c[:, C_MASK:C_MASK + SEQ] = 1.0
    c[:, C_MASK:C_MASK + P] = col >= row
    c[:, C_BEFORE:C_BEFORE + P] = row < col
    c[:, C_REV:C_REV + E * TILES] = np.repeat(E - np.arange(E), TILES)
    c[:, C_TILE:C_ALL] = np.repeat(np.arange(EXPERT_TILES), E)
    cols = [a(f"attn_b1{n}") for n in "qkv"] + [a("attn_b2q"), a("attn_b2k")]
    cols = np.concatenate([np.stack(cols), a("ffn_bs1").reshape(-1, P), a("ffn_be1").reshape(-1, P)])
    rows = np.concatenate([a("ffn_br"), a("attn_b2v"), a("attn_ln_w"), a("attn_ln_b"), a("ffn_bs2"), a("ffn_be2").reshape(-1)])
    arrays = {
        "x": a("attn_x"), "w1": np.stack([a(f"attn_W1{n}") for n in "qkv"]), "w2": np.stack([a(f"attn_W2{n}") for n in "qkv"]),
        "ws1": a("ffn_Ws1"), "ws2": a("ffn_Ws2"), "we1": a("ffn_We1"), "we2": a("ffn_We2"), "wr": a("ffn_Wr"), "consts": c,
        "bias_cols": np.ascontiguousarray(cols.T), "bias_rows": np.ascontiguousarray(np.broadcast_to(rows[None, :], (P, rows.size))),
    }
    nc = bacc.Bacc("TRN2", target_bir_lowering=False, num_devices=1)
    args = [nc.dram_tensor(f"in_{n}", v.shape, mybir.dt.from_np(v.dtype), kind="ExternalInput").ap() for n, v in arrays.items()]
    out = nc.dram_tensor("out_0", (BATCH, SEQ, D), mybir.dt.float32, kind="ExternalOutput").ap()
    block_kernel(nc, *args, out)
    r = run_bass_kernel_spmd(nc, [{f"in_{n}": v for n, v in arrays.items()}], core_ids=[0])
    return r.results[0]["out_0"]
```

```python
import concourse.bass as bass
from concourse import mybir
from contextlib import ExitStack

P = 128
BATCH, SEQ, D = 8, 512, 128
TOKENS = BATCH * SEQ
TPB = SEQ // P
TILES = TOKENS // P
E, TOP = 12, 2
HS, HR = 2 * D, 3 * D
CS, CR = HS // P, HR // P
SLOTS = 256
SUB = SLOTS // P
EXPERT_TILES = (TOP * TOKENS + E * (SLOTS - 1)) // SLOTS
ALL_SLOTS = EXPERT_TILES * SLOTS
SUBTILES = ALL_SLOTS // P
EPS = 1e-5
INV_SCALE = 1.0 / float(128 * 256) ** 0.5
INV_TAU = 1.0 / 1.5
MASKED = -3.0e38
ASSIGN = TOP * TILES
ET = E * TILES

PAIRS = BATCH // 2
E_PAIRS = EXPERT_TILES // 2
CHUNK = 16
INV_STEPS = ASSIGN // CHUNK
RING = 2

C_ID = 0
C_MASK = C_ID + P
C_BEFORE = C_MASK + SEQ
C_REV = C_BEFORE + P
C_TILE = C_REV + ET
C_IOTA = C_TILE + EXPERT_TILES * E
C_TOKEN = C_IOTA + P
C_ALL = C_TOKEN + ASSIGN

B_1 = 0
B_2 = 3
B_S1 = 5
B_ALL = B_S1 + 2 * CS

R_BR = 0
R_B2V = R_BR + E
R_LNW = R_B2V + D
R_LNB = R_LNW + D
R_BS2 = R_LNB + D
R_ALL = R_BS2 + D

W1_ALL = 2 * HR + 2 * CR
W2_ALL = CR * D + D


def block_kernel(nc, x, w1, w2, ws1, ws2, expert1, expert2, wr, consts, bias_cols, bias_rows, out):
    fp32, fp32r, fp16 = mybir.dt.float32, mybir.dt.float32r, mybir.dt.float16
    i32, u32 = mybir.dt.int32, mybir.dt.uint32
    ALU, ACT, AX = mybir.AluOpType, mybir.ActivationFunctionType, mybir.AxisListType
    ds = bass.ds

    x_tiled = x.rearrange("b (t p) d -> p (b t) d", p=P)
    out_tiled = out.rearrange("b (t p) d -> p (b t) d", p=P)
    xn_rows = nc.dram_tensor("xn_rows", [TOKENS, D], fp32, kind="Internal").ap()
    slot_y = nc.dram_tensor("slot_y", [ALL_SLOTS, D], fp32, kind="Internal").ap()
    xn_tiled = xn_rows.rearrange("(t p) d -> p t d", p=P)
    slot_y_tiled = slot_y.rearrange("(t p) d -> p t d", p=P)
    expert1_rows = expert1.rearrange("e p h -> (e p) h")
    expert2_rows = expert2.rearrange("e p h -> (e p) h")

    ctx = ExitStack()
    with ctx:
        def sb(name, shape, dt=fp32):
            return ctx.enter_context(nc.sbuf_tensor(name, shape, dt))

        def sem(name):
            return ctx.enter_context(nc.semaphore(name))

        def sems(*names):
            return [sem(n) for n in names]

        x_all = sb("x_all", [P, TILES, D])
        xT_hi, xT_lo = sb("xT_hi", [P, TOKENS], fp32r), sb("xT_lo", [P, TOKENS], fp32r)
        qT_all = sb("qT_all", [P, TOKENS])
        kT_all = sb("kT_all", [P, TOKENS])
        v_all = sb("v_all", [P, TILES, D])
        acc = sb("acc", [P, TILES, D])
        on_all = x_all

        w1_sb = sb("w1_sb", [P, 3 * D])
        w1_hi, w1_lo = sb("w1_hi", [P, 3 * D], fp32r), sb("w1_lo", [P, 3 * D], fp32r)
        w2_sb = sb("w2_sb", [P, 3, D])
        ws1_sb = sb("ws1_sb", [P, 2 * HS])
        ws1_hi, ws1_lo = sb("ws1_hi", [P, 2 * HS], fp32r), sb("ws1_lo", [P, 2 * HS], fp32r)
        ws2_sb = sb("ws2_sb", [P, CS, D])
        wr_sb = sb("wr_sb", [P, E])
        cst = sb("cst", [P, C_ALL])
        bcol = sb("bcol", [P, B_ALL])
        brow = sb("brow", [P, R_ALL])
        ident = cst[:, C_ID:C_ID + P]
        mask = cst[:, C_MASK:C_MASK + SEQ]
        rev = cst[:, C_REV:C_REV + ET]
        tile_no = cst[:, C_TILE:C_TILE + EXPERT_TILES * E]
        token = cst[:, C_TOKEN:C_TOKEN + ASSIGN]
        before16, ones16, zeros16, iota16 = (sb(n, [P, P], fp16) for n in ("before16", "ones16", "zeros16", "iota16"))
        qbias = sb("qbias", [P, 1])
        lnb_bs2 = sb("lnb_bs2", [P, D])
        half_neg = sb("half_neg", [P, TILES])

        x_stats = sb("x_stats", [P, TILES, 6])
        x_mean, x_rstd, x_shift = (sb(n, [P, TILES]) for n in ("x_mean", "x_rstd", "x_shift"))
        var_eps, diff = sb("var_eps", [P, TILES]), sb("diff", [P, TILES])
        xn_st = sb("xn_st", [P, 2, TPB, D])
        xnT_st = sb("xnT_st", [P, 2, SEQ])

        scratch = sb("scratch", [P, 9 * ET])
        lg, lg2, hit, total, cum, pos, ones_et = (scratch[:, n * ET:(n + 1) * ET] for n in range(7))
        picked = hit
        best = sb("best", [P, TOP, TILES])
        first = sb("first", [P, TILES])
        choice = scratch[:, 7 * ET:9 * ET].rearrange("p (k n) -> p k n", k=TOP)
        taken = sb("taken", [P, ET], fp16)
        cnt_f, tiles_f, tile_end, run_off = (sb(n, [P, E]) for n in ("cnt_f", "tiles_f", "tile_end", "run_off"))
        cnt_i, tiles_i = sb("cnt_i", [P, E], i32), sb("tiles_i", [P, E], i32)
        slot_f = sb("slot_f", [P, TOP, TILES])
        slot = sb("slot", [P, TOP, TILES], u32)
        ended = scratch[:, 2 * W1_ALL:2 * W1_ALL + EXPERT_TILES * E]
        owner_f = sb("owner_f", [P, EXPERT_TILES])
        owner = sb("owner", [P, EXPERT_TILES], i32)
        gap, ratio, denom = (sb(n, [P, TILES]) for n in ("gap", "ratio", "denom"))
        weight = sb("weight", [P, TOP, TILES])

        h_sb = sb("h_sb", [P, 2, SEQ])
        kT_st = h_sb
        gate_sb = sb("gate_sb", [P, 2, SEQ])
        sT = sb("sT", [P, 2, TPB, SEQ])
        act_sb = sT[:, 1, :, :].rearrange("p (u c) s -> p u c s", u=2)
        eact = sT[:, 0, 0:CR, :].rearrange("p c (u s) -> p u c s", u=2)

        slot_i, high_i, low_i = (sb(n, [P, ASSIGN], i32) for n in ("slot_i", "high_i", "low_i"))
        high, low16 = sb("high", [P, ASSIGN]), sb("low16", [P, ASSIGN], fp16)
        high_st, token_st = sb("high_st", [P, 2, CHUNK]), sb("token_st", [P, 2, CHUNK])
        low_hot = sT[:, 0, :, :].rearrange("p t s -> p (t s)").bitcast(fp16).rearrange("p (u c r) -> p u c r", u=2, r=P)
        high_token = sT[:, 1, :, :].rearrange("p t s -> p (t s)").bitcast(fp16)[:, 0:2 * CHUNK * SUBTILES].rearrange(
            "p (u c a) -> p u c a", u=2, a=SUBTILES)
        slot_token = sb("slot_token", [P, SUBTILES], u32)

        e1_sb = scratch[:, 0:2 * W1_ALL].rearrange("p (u n) -> p u n", u=2)
        e1_hi, e1_lo = sb("e1_hi", [P, 2, 2 * HR], fp32r), sb("e1_lo", [P, 2, 2 * HR], fp32r)
        eb1 = sb("eb1", [P, 2, 2 * CR])
        e2_sb = xnT_st
        eb2 = e2_sb[:, :, CR * D:W2_ALL]
        idx_st = sb("idx_st", [P, 2, SUB], u32)
        xs_sb = xn_st[:, :, 0:SUB, :]
        xsT_hi, xsT_lo = sb("xsT_hi", [P, 2, SLOTS], fp32r), sb("xsT_lo", [P, 2, SLOTS], fp32r)
        egate = gate_sb[:, :, 0:SLOTS]
        ys_sb = h_sb[:, 0, :].rearrange("p (u s d) -> p u s d", u=2, d=D)
        o_stats = sb("o_stats", [P, 2 * TPB, 6])
        o_mean, o_rstd, o_shift, o_var_eps, o_diff = (sb(n, [P, 2 * TPB]) for n in ("o_mean", "o_rstd", "o_shift", "o_var_eps", "o_diff"))
        y_st = scratch[:, 0:2 * TOP * SEQ].rearrange("p (u k t d) -> p u k t d", u=2, k=TOP, d=D)
        yidx_st = sb("yidx_st", [P, 2, TOP, TPB], u32)

        bank = [ctx.enter_context(nc.psum_tensor(f"bank{i}", [P, 512], fp32)) for i in range(8)]

        const_in, bias_in, w_in = sems("const_in", "bias_in", "w_in")
        x_in = [sem(f"x_in{q}") for q in range(4)]
        set_up, cast, w_high, w_low = sems("set_up", "cast", "w_high", "w_low")
        a_stat, a_step, a_var, a_rstd, a_shift = sems("a_stat", "a_step", "a_var", "a_rstd", "a_shift")
        a_xn, a_xn_act, a_tr, a_st, a_hi, a_lo, a_lg = sems("a_xn", "a_xn_act", "a_tr", "a_st", "a_hi", "a_lo", "a_lg")
        a_keep = sems("a_keep0", "a_keep1")
        b_h, b_gelu, b_o, b_evac = sems("b_h", "b_gelu", "b_o", "b_evac")
        r_step, r_taken, r_rank, r_slot, r_split, r_owner, r_gap, r_exp = sems(
            "r_step", "r_taken", "r_rank", "r_slot", "r_split", "r_owner", "r_gap", "r_exp")
        i_st, i_high, i_mm, i_done, i_map = sems("i_st", "i_high", "i_mm", "i_done", "i_map")
        e_x, e_w1, e_w2, e_st = (sems(f"{n}0", f"{n}1") for n in ("e_x", "e_w1", "e_w2", "e_st"))
        e_idx, e_tr, e_xhi, e_xlo, e_whi, e_wlo = sems("e_idx", "e_tr", "e_xhi", "e_xlo", "e_whi", "e_wlo")
        e_g, e_a, e_gate, e_act, e_y, e_yev = sems("e_g", "e_a", "e_gate", "e_act", "e_y", "e_yev")
        e_side, wait_holder = sems("e_side", "wait_holder")
        c_k, c_s, c_mask, c_o, c_stat, c_step, c_var, c_rstd, c_shift, c_on = sems(
            "c_k", "c_s", "c_mask", "c_o", "c_stat", "c_step", "c_var", "c_rstd", "c_shift", "c_on")
        d_g, d_a, d_gate, d_act, d_y, d_acc = sems("d_g", "d_a", "d_gate", "d_act", "d_y", "d_acc")
        gathered = sems("gathered0", "gathered1")
        f_idx, f_weight, f_w, f_res, f_scaled, f_y0, f_done, stored = sems(
            "f_idx", "f_weight", "f_w", "f_res", "f_scaled", "f_y0", "f_done", "stored")

        B_ITEMS, D_ITEMS = 3 * BATCH, CS * BATCH
        SIDE_PAIRS = TILES // 2
        QT = TILES // 4
        HALF = TILES // 2

        block = ctx.enter_context(nc.Block())

        @block.sync
        def _(sp):
            for s in (*e_st, *a_keep):
                sp.sem_inc(s, 16)
            for q in range(4):
                sp.dma_start(x_all[:, q * QT:(q + 1) * QT, :], x_tiled[:, q * QT:(q + 1) * QT, :]).then_inc(x_in[q], 16)
            sp.dma_start(cst[:, :], consts).then_inc(const_in, 16)
            sp.dma_start(wr_sb[:, :], wr).then_inc(bias_in, 16)
            sp.dma_start(brow[:, :], bias_rows).then_inc(bias_in, 16)
            sp.dma_start(bcol[:, :], bias_cols).then_inc(bias_in, 16)
            for n in range(3):
                sp.dma_start(w1_sb[:, n * D:(n + 1) * D], w1[n]).then_inc(w_in, 16)
                sp.dma_start(w2_sb[:, n, :], w2[n]).then_inc(w_in, 16)
            sp.dma_start(ws1_sb[:, :], ws1).then_inc(w_in, 16)
            sp.dma_start(ws2_sb[:, :, :], ws2.rearrange("(c p) d -> p c d", p=P)).then_inc(w_in, 16)
            with sp.Fori(0, PAIRS) as i:
                for u in range(2):
                    b = 2 * i + u
                    sp.wait_ge(a_xn, b + 1 + RING)
                    sp.sem_inc(wait_holder, 1)
                    sp.wait_ge(a_xn_act, b + 1)
                    sp.wait_ge(a_keep[u], 16 * i + 16)
                    sp.dma_start(xn_tiled[:, ds(b * TPB, TPB), :], xn_st[:, u, :, :]).then_inc(a_keep[u], 16)

            def load(j, u):
                e = sp.value_load(owner[0:1, ds(j, 1)], min_val=0, max_val=E - 1)
                sp.wait_ge(e_wlo, j + 1)
                sp.sem_inc(wait_holder, 1)
                sp.dma_start(e1_sb[:, u, :], expert1_rows[ds(e * P, P), :]).then_inc(e_w1[u], 16)
                sp.wait_ge(e_yev, j + 1)
                sp.sem_inc(wait_holder, 1)
                sp.dma_start(e2_sb[:, u, :], expert2_rows[ds(e * P, P), :]).then_inc(e_w2[u], 16)

            def store(j, u):
                sp.wait_ge(e_yev, j + 1 + RING)
                sp.dma_start(slot_y_tiled[:, ds(j * SUB, SUB), :], ys_sb[:, u, :, :]).then_inc(e_st[u], 16)

            sp.wait_ge(r_owner, 1)
            sp.wait_ge(a_lo, BATCH + RING)
            load(0, 0)
            load(1, 1)
            with sp.Fori(0, E_PAIRS - 1) as i:
                for u in range(2):
                    load(2 * i + u + 2, u)
                    store(2 * i + u, u)
            load(EXPERT_TILES - 1, 0)
            for j in range(EXPERT_TILES - 3, EXPERT_TILES):
                store(j, j % 2)

            with sp.Fori(0, BATCH) as b:
                sp.wait_ge(f_done, b + 1 + RING)
                sp.dma_start(out_tiled[:, ds(b * TPB, TPB), :], acc[:, ds(b * TPB, TPB), :]).then_inc(stored, 16)
            sp.wait_ge(stored, 16 * BATCH)

        @block.gpsimd
        def _(pool):
            pool.sem_inc(a_lo, RING)
            nc.gpsimd.memset(half_neg[:, :], -0.5).then_inc(set_up, 1)
            nc.gpsimd.memset(ones16[:, :], 1.0).then_inc(set_up, 1)
            nc.gpsimd.memset(zeros16[:, :], 0.0).then_inc(set_up, 1)
            nc.gpsimd.memset(ones_et[:, :], 1.0).then_inc(set_up, 1)
            pool.wait_ge(set_up, 4)
            for h in range(2):
                at = slice(h * HALF, (h + 1) * HALF)
                pool.wait_ge(a_var, h + 1)
                nc.gpsimd.tensor_tensor(x_rstd[:, at], var_eps[:, at], half_neg[:, at], ALU.pow).then_inc(a_rstd, 1)
            with pool.Fori(0, PAIRS) as i:
                for u in range(2):
                    b = 2 * i + u
                    pool.wait_ge(a_hi, b + 1 + RING)
                    nc.gpsimd.tensor_tensor(xT_lo[:, ds(b * SEQ, SEQ)], xnT_st[:, u, :],
                                            xT_hi[:, ds(b * SEQ, SEQ)].bitcast(fp32), ALU.subtract).then_inc(a_lo, 1)
            pool.wait_ge(w_high, 2)
            nc.gpsimd.tensor_tensor(w1_lo[:, :], w1_sb[:, :], w1_hi[:, :].bitcast(fp32), ALU.subtract).then_inc(w_low, 1)
            nc.gpsimd.tensor_tensor(ws1_lo[:, :], ws1_sb[:, :], ws1_hi[:, :].bitcast(fp32), ALU.subtract).then_inc(w_low, 1)

            def gather_rows(j, u):
                pool.wait_ge(e_tr, j + 1)
                nc.gpsimd.tensor_copy(idx_st[:, u, :], slot_token[:, ds(j * SUB, SUB)]).then_inc(e_idx, 1)
                pool.wait_ge(e_idx, j + 1)
                pool.sem_inc(wait_holder, 1)
                for s in range(SUB):
                    nc.gpsimd.indirect_dma_start(xs_sb[:, u, s, :], None, xn_rows,
                                                 bass.IndirectOffsetOnAxis(ap=idx_st[:, u, s:s + 1], axis=0)).then_inc(e_x[u], 16)

            def prepare(i):
                at = ds(2 * i, 2)
                nc.gpsimd.tensor_tensor(acc[:, at, :], x_all[:, at, :], lnb_bs2[:, :].unsqueeze(1).to_broadcast([P, 2, D]),
                                        ALU.add).then_inc(e_side, 1)
                nc.gpsimd.tensor_tensor(v_all[:, at, :], v_all[:, at, :],
                                        brow[:, R_B2V:R_B2V + D].unsqueeze(1).to_broadcast([P, 2, D]), ALU.add).then_inc(e_side, 1)

            pool.wait_ge(i_map, 1)
            for u in range(2):
                pool.wait_ge(a_keep[u], 16 * PAIRS + 16)
            pool.wait_ge(b_evac, B_ITEMS + RING)
            with pool.Fori(0, SIDE_PAIRS) as i:
                for u in range(2):
                    gather_rows(2 * i + u, u)
                prepare(i)
            with pool.Fori(SIDE_PAIRS, E_PAIRS) as i:
                for u in range(2):
                    gather_rows(2 * i + u, u)
            gather_rows(EXPERT_TILES - 1, 0)

            def gather_back(b, u):
                pool.wait_ge(f_done, b + 1)
                nc.gpsimd.tensor_copy(yidx_st[:, u, :, :], slot[:, :, ds(b * TPB, TPB)]).then_inc(f_idx, 1)
                pool.wait_ge(f_idx, b + 1)
                pool.sem_inc(wait_holder, 1)
                for k in range(TOP):
                    for t in range(TPB):
                        nc.gpsimd.indirect_dma_start(y_st[:, u, k, t, :], None, slot_y,
                                                     bass.IndirectOffsetOnAxis(ap=yidx_st[:, u, k, t:t + 1], axis=0)
                                                     ).then_inc(gathered[u], 16)

            pool.wait_ge(e_st[0], 16 * (EXPERT_TILES - E_PAIRS) + 16)
            pool.wait_ge(e_st[1], 16 * E_PAIRS + 16)
            with pool.Fori(0, PAIRS) as i:
                gather_back(2 * i, 0)
                pool.wait_ge(c_var, i + 1)
                nc.gpsimd.tensor_tensor(o_rstd[:, :], o_var_eps[:, :], half_neg[:, 0:2 * TPB], ALU.pow).then_inc(c_rstd, 1)
                gather_back(2 * i + 1, 1)

        @block.scalar
        def _(act):
            for s in (a_st, a_hi, b_gelu, b_evac, e_xhi, e_gate, c_on, d_gate):
                act.sem_inc(s, RING)
            for h in range(2):
                act.wait_ge(a_shift, h + 1)
                with act.Fori(h * PAIRS // 2, (h + 1) * PAIRS // 2) as i:
                    for u in range(2):
                        b = 2 * i + u
                        t = b * TPB + TPB - 1
                        act.wait_ge(a_tr, b + 1)
                        act.wait_ge(a_keep[u], 16 * i + 16)
                        nc.scalar.activation(xn_st[:, u, TPB - 1, :], x_all[:, ds(t, 1), :].rearrange("p a d -> p (a d)"), ACT.Identity,
                                             bias=x_shift[:, ds(t, 1)], scale=x_rstd[:, ds(t, 1)]).then_inc(a_xn_act, 1)
                    for u in range(2):
                        b = 2 * i + u
                        act.wait_ge(a_tr, b + 1 + RING)
                        act.wait_ge(a_lg, b + 1)
                        act.wait_ge(a_lo, b + 1)
                        nc.scalar.activation(xnT_st[:, u, :], bank[4 + u][:, :], ACT.Copy).then_inc(a_st, 1)
                        nc.scalar.activation(xT_hi[:, ds(b * SEQ, SEQ)], bank[4 + u][:, :], ACT.Copy).then_inc(a_hi, 1)
            act.wait_ge(w_in, 16 * 8)
            nc.scalar.activation(w1_hi[:, :], w1_sb[:, :], ACT.Copy).then_inc(w_high, 1)
            nc.scalar.activation(ws1_hi[:, :], ws1_sb[:, :], ACT.Copy).then_inc(w_high, 1)
            act.wait_ge(bias_in, 48)
            nc.scalar.mul(qbias[:, :], bcol[:, B_2:B_2 + 1], INV_SCALE).then_inc(w_high, 1)
            act.wait_ge(w_high, 3)

            def gelu(m, n, h):
                act.wait_ge(b_h, m + 1)
                act.wait_ge(b_o, m + 1)
                nc.scalar.activation(h_sb[:, h, :], bank[h][:, :], ACT.Gelu, bias=bcol[:, B_1 + n:B_1 + n + 1]).then_inc(b_gelu, 1)

            def evac(m, b, n, h):
                act.wait_ge(b_o, m + 1 + RING)
                if n == 0:
                    nc.scalar.activation(qT_all[:, ds(b * SEQ, SEQ)], bank[2 + h][:, :], ACT.Identity,
                                         bias=qbias[:, :], scale=INV_SCALE).then_inc(b_evac, 1)
                elif n == 1:
                    nc.scalar.activation(kT_all[:, ds(b * SEQ, SEQ)], bank[2 + h][:, :], ACT.Identity,
                                         bias=bcol[:, B_2 + 1:B_2 + 2]).then_inc(b_evac, 1)
                else:
                    nc.scalar.activation(v_all[:, ds(b * TPB, TPB), :],
                                         bank[2 + h][:, :].rearrange("p (t d) -> p t d", d=D), ACT.Copy).then_inc(b_evac, 1)

            def qkv_pair(i):
                for k in range(6):
                    gelu(6 * i + k, k % 3, k % 2)
                    if k:
                        evac(6 * i + k - 1, 2 * i + (k - 1) // 3, (k - 1) % 3, (k - 1) % 2)
                evac(6 * i + 5, 2 * i + 1, 2, 1)

            qkv_pair(0)
            with act.Fori(1, PAIRS) as i:
                qkv_pair(i)

            act.wait_ge(r_gap, 1)
            nc.scalar.activation(ratio[:, :], gap[:, :], ACT.Exp, scale=INV_TAU).then_inc(r_exp, 1)

            THIRD = 2 * HR // CR

            def weight_high(j, u, pair, c):
                if c == 0:
                    act.wait_ge(e_w1[u], 16 * pair + 16)
                    act.wait_ge(e_y, j + 1)
                at = slice(c * THIRD, (c + 1) * THIRD)
                nc.scalar.activation(e1_hi[:, u, at], e1_sb[:, u, at], ACT.Copy).then_inc(e_whi, 1)

            def rows_high(j, u):
                act.wait_ge(e_tr, j + 1 + RING)
                nc.scalar.activation(xsT_hi[:, u, :], bank[2 + u][:, 0:SLOTS], ACT.Copy).then_inc(e_xhi, 1)

            def expert_gates(j, u, next_pair):
                for c in range(CR):
                    m = CR * j + c
                    g = (CR * u + c) % 2
                    act.wait_ge(e_g, m + 1)
                    act.wait_ge(e_act, m + 1)
                    nc.scalar.activation(egate[:, g, :], bank[4 + g][:, 0:SLOTS], ACT.Gelu,
                                         bias=eb1[:, u, CR + c:CR + c + 1]).then_inc(e_gate, 1)
                    if next_pair is not None:
                        weight_high(j + 1, 1 - u, next_pair, c)
                if next_pair is not None:
                    rows_high(j + 1, 1 - u)

            for c in range(CR):
                weight_high(0, 0, 0, c)
            rows_high(0, 0)
            with act.Fori(0, E_PAIRS) as i:
                for u in range(2):
                    expert_gates(2 * i + u, u, i + u)
            expert_gates(EXPERT_TILES - 1, 0, None)

            def y_scale(b, u):
                act.wait_ge(gathered[u], 16 * TOP * TPB * (b // 2 + 1) if isinstance(b, int) else 16 * TOP * TPB * (turn[0] + 1))
                for k in range(TOP):
                    for t in range(TPB):
                        last = nc.scalar.activation(y_st[:, u, k, t, :], y_st[:, u, k, t, :], ACT.Copy,
                                                    scale=weight[:, k, ds(b * TPB + t, 1)])
                last.then_inc(f_scaled, 1)

            turn = [None]
            act.wait_ge(f_weight, 1)
            act.wait_ge(e_st[0], 16 * (EXPERT_TILES - E_PAIRS) + 16)
            act.wait_ge(e_st[1], 16 * E_PAIRS + 16)
            act.wait_ge(e_side, 2 * SIDE_PAIRS)
            with act.Fori(0, PAIRS) as i:
                turn[0] = i
                for u in range(2):
                    b = 2 * i + u
                    act.wait_ge(c_o, b + 1)
                    nc.scalar.activation(kT_st[:, u, :], kT_all[:, ds(b * SEQ, SEQ)], ACT.Copy).then_inc(c_k, 1)
                for k in range(2 * CS):
                    m = 2 * CS * i + k
                    c = k % CS
                    act.wait_ge(d_g, m + 1)
                    act.wait_ge(d_act, m + 1)
                    nc.scalar.activation(gate_sb[:, k % 2, :], bank[4 + k % 2][:, :], ACT.Gelu,
                                         bias=bcol[:, B_S1 + CS + c:B_S1 + CS + c + 1]).then_inc(d_gate, 1)
                    if k == 0:
                        act.wait_ge(c_shift, i + 1)
                        for u in range(2):
                            for t in range(TPB):
                                s = u * TPB + t
                                last = nc.scalar.activation(on_all[:, ds((2 * i + u) * TPB + t, 1), :].rearrange("p a d -> p (a d)"),
                                                            bank[u][:, t * D:(t + 1) * D], ACT.Identity,
                                                            bias=o_shift[:, s:s + 1], scale=o_rstd[:, s:s + 1])
                            last.then_inc(c_on, 1)
                y_scale(2 * i, 0)
                y_scale(2 * i + 1, 1)

        @block.vector
        def _(dve):
            steps = [0]

            def step(ins):
                steps[0] += 1
                ins.then_inc(r_step, 1)
                dve.wait_ge(r_step, steps[0])

            def moments(stats, mean, var, dif, counter, base, made):
                even, odd = stats[:, :, 1], stats[:, :, 4]
                nc.vector.tensor_tensor(mean, even, odd, ALU.add).then_inc(counter, 1)
                nc.vector.tensor_tensor(dif, even, odd, ALU.subtract).then_inc(counter, 1)
                nc.vector.tensor_tensor(var, stats[:, :, 2], stats[:, :, 5], ALU.add).then_inc(counter, 1)
                dve.wait_ge(counter, base + 3)
                nc.vector.tensor_tensor(dif, dif, dif, ALU.mult).then_inc(counter, 1)
                nc.vector.tensor_scalar(var, var, 1.0 / D, EPS, ALU.mult, ALU.add).then_inc(counter, 1)
                nc.vector.tensor_scalar(mean, mean, 0.5, None, ALU.mult).then_inc(counter, 1)
                dve.wait_ge(counter, base + 6)
                nc.vector.scalar_tensor_tensor(var, dif, 0.25, var, ALU.mult, ALU.add).then_inc(made, 1)

            for s in (a_xn, e_act, e_wlo, e_xlo, e_yev, c_mask, d_act, d_acc, f_done):
                dve.sem_inc(s, RING)
            for h in range(2):
                for q in (2 * h, 2 * h + 1):
                    dve.wait_ge(x_in[q], 16)
                    with dve.Fori(q * QT // 2, (q + 1) * QT // 2) as t:
                        for s in range(2):
                            last = nc.vector.bn_stats(x_stats[:, ds(2 * t + s, 1), :].rearrange("p a d -> p (a d)"),
                                                      x_all[:, ds(2 * t + s, 1), :].rearrange("p a d -> p (a d)"))
                        last.then_inc(a_stat, 1)
                dve.wait_ge(a_stat, (h + 1) * HALF // 2)
                at = slice(h * HALF, (h + 1) * HALF)
                moments(x_stats[:, at, :], x_mean[:, at], var_eps[:, at], diff[:, at], a_step, 6 * h, a_var)
            for h in range(2):
                at = slice(h * HALF, (h + 1) * HALF)
                dve.wait_ge(a_rstd, h + 1)
                nc.vector.scalar_tensor_tensor(x_shift[:, at], x_mean[:, at], -1.0, x_rstd[:, at], ALU.mult, ALU.mult).then_inc(a_shift, 1)
                with dve.Fori(h * PAIRS // 2, (h + 1) * PAIRS // 2) as i:
                    for u in range(2):
                        b = 2 * i + u
                        dve.wait_ge(a_tr, b + 1)
                        dve.wait_ge(a_keep[u], 16 * i + 16)
                        for t in range(TPB - 1):
                            last = nc.vector.tensor_scalar(xn_st[:, u, t, :],
                                                           x_all[:, ds(b * TPB + t, 1), :].rearrange("p a d -> p (a d)"),
                                                           x_mean[:, ds(b * TPB + t, 1)], x_rstd[:, ds(b * TPB + t, 1)],
                                                           ALU.subtract, ALU.mult)
                        last.then_inc(a_xn, 1)
            dve.wait_ge(const_in, 16)
            dve.wait_ge(bias_in, 48)
            nc.vector.tensor_copy(before16[:, :], cst[:, C_BEFORE:C_BEFORE + P]).then_inc(cast, 1)
            nc.vector.tensor_copy(iota16[:, :], cst[:, C_IOTA:C_IOTA + P]).then_inc(cast, 1)
            nc.vector.tensor_tensor(lnb_bs2[:, :], brow[:, R_LNB:R_LNB + D], brow[:, R_BS2:R_BS2 + D], ALU.add).then_inc(cast, 1)

            def et(ap):
                return ap.rearrange("p (e t) -> p e t", t=TILES)

            def te(ap):
                return ap.rearrange("p (e t) -> p t e", t=TILES)

            def over_e(ap):
                return ap.unsqueeze(1).to_broadcast([P, E, TILES])

            def over_t(ap):
                return ap.unsqueeze(2).to_broadcast([P, E, TILES])

            dve.wait_ge(a_lg, BATCH + RING)
            step(nc.vector.tensor_tensor(et(lg[:, :]), bank[6][:, 0:ET].rearrange("p (t e) -> p e t", e=E),
                                         over_t(brow[:, R_BR:R_BR + E]), ALU.add))
            src = lg
            for k in range(TOP):
                step(nc.vector.tensor_reduce(best[:, k, :], te(src[:, :]), AX.X, ALU.max))
                step(nc.vector.tensor_tensor(et(hit[:, :]), et(src[:, :]), over_e(best[:, k, :]), ALU.is_equal))
                step(nc.vector.tensor_tensor(hit[:, :], hit[:, :], rev, ALU.mult))
                step(nc.vector.tensor_reduce(first[:, :], te(hit[:, :]), AX.X, ALU.max))
                step(nc.vector.tensor_tensor(et(choice[:, k, :]), et(rev), over_e(first[:, :]), ALU.is_equal))
                if k == 0:
                    step(nc.vector.scalar_tensor_tensor(lg2[:, :], choice[:, 0, :], MASKED, lg[:, :], ALU.mult, ALU.add))
                    src = lg2
            nc.vector.tensor_tensor(taken[:, :], choice[:, 0, :], choice[:, 1, :], ALU.add).then_inc(r_taken, 1)
            nc.vector.tensor_tensor(gap[:, :], best[:, 1, :], best[:, 0, :], ALU.subtract).then_inc(r_gap, 1)
            dve.wait_ge(set_up, 4)
            dve.wait_ge(r_rank, 2)
            step(nc.vector.tensor_copy(total[:, :], bank[7][:, 0:ET]))
            step(nc.vector.tensor_tensor_scan(cum[:, :], ones_et[:, :], total[:, :], 0.0, ALU.mult, ALU.add))
            step(nc.vector.tensor_tensor(total[:, :], cum[:, :], total[:, :], ALU.subtract))
            step(nc.vector.tensor_tensor(cnt_f[:, :], et(cum[:, :])[:, :, TILES - 1], et(total[:, :])[:, :, 0], ALU.subtract))
            step(nc.vector.tensor_scalar(cnt_i[:, :], cnt_f[:, :], float(SLOTS - 1), None, ALU.add))
            step(nc.vector.tensor_scalar(tiles_i[:, :], cnt_i[:, :], SLOTS.bit_length() - 1, None, ALU.arith_shift_right))
            step(nc.vector.tensor_copy(tiles_f[:, :], tiles_i[:, :]))
            step(nc.vector.tensor_tensor_scan(tile_end[:, :], ones_et[:, 0:E], tiles_f[:, :], 0.0, ALU.mult, ALU.add))
            step(nc.vector.tensor_tensor(run_off[:, :], tile_end[:, :], tiles_f[:, :], ALU.subtract))
            step(nc.vector.scalar_tensor_tensor(run_off[:, :], run_off[:, :], float(SLOTS), et(total[:, :])[:, :, 0],
                                                ALU.mult, ALU.subtract))
            step(nc.vector.tensor_tensor(pos[:, :], total[:, :], bank[6][:, 0:ET], ALU.add))
            step(nc.vector.tensor_tensor(et(pos[:, :]), et(pos[:, :]), over_t(run_off[:, :]), ALU.add))
            for k in range(TOP):
                step(nc.vector.tensor_tensor(picked[:, :], choice[:, k, :], pos[:, :], ALU.mult))
                step(nc.vector.tensor_reduce(slot_f[:, k, :], te(picked[:, :]), AX.X, ALU.add))
            slots = slot_f[:, :, :].rearrange("p k t -> p (k t)")
            step(nc.vector.tensor_copy(slot_i[:, :], slots))
            nc.vector.tensor_scalar(low_i[:, :], slot_i[:, :], P - 1, None, ALU.bitwise_and).then_inc(r_step, 1)
            step(nc.vector.tensor_scalar(high_i[:, :], slot_i[:, :], P.bit_length() - 1, None, ALU.arith_shift_right))
            steps[0] += 1
            dve.wait_ge(r_step, steps[0])
            nc.vector.tensor_copy(low16[:, :], low_i[:, :]).then_inc(r_split, 1)
            nc.vector.tensor_copy(high[:, :], high_i[:, :]).then_inc(r_split, 1)
            nc.vector.tensor_copy(slot[:, :, :], slot_f[:, :, :]).then_inc(r_slot, 1)

            dve.wait_ge(r_split, 2)
            with dve.Fori(0, INV_STEPS // 2) as i:
                for u in range(2):
                    q = 2 * i + u
                    dve.wait_ge(i_mm, q + 1)
                    nc.vector.tensor_copy(high_st[:, u, :], high[:, ds(q * CHUNK, CHUNK)]).then_inc(i_st, 1)
                    nc.vector.tensor_copy(token_st[:, u, :], token[:, ds(q * CHUNK, CHUNK)]).then_inc(i_st, 1)
                    nc.vector.tensor_tensor(low_hot[:, u, :, :], iota16[:, :].unsqueeze(1).to_broadcast([P, CHUNK, P]),
                                            low16[:, ds(q * CHUNK, CHUNK)].unsqueeze(2).to_broadcast([P, CHUNK, P]),
                                            ALU.is_equal)
                    dve.wait_ge(i_st, 2 * q + 2)
                    for c in range(CHUNK):
                        last = nc.vector.tensor_scalar(high_token[:, u, c, :], iota16[:, 0:SUBTILES], high_st[:, u, c:c + 1],
                                                       token_st[:, u, c:c + 1], ALU.is_equal, ALU.mult)
                    last.then_inc(i_high, 1)
            step(nc.vector.tensor_tensor(ended[:, :].rearrange("p (j e) -> p j e", e=E),
                                         tile_end[:, :].unsqueeze(1).to_broadcast([P, EXPERT_TILES, E]),
                                         tile_no.rearrange("p (j e) -> p j e", e=E), ALU.is_le))
            step(nc.vector.tensor_reduce(owner_f[:, :], ended[:, :].rearrange("p (j e) -> p j e", e=E), AX.X, ALU.add))
            nc.vector.tensor_scalar(owner[:, :], owner_f[:, :], float(E - 1), None, ALU.min).then_inc(r_owner, 1)
            dve.wait_ge(i_done, 1)
            nc.vector.tensor_scalar(slot_token[:, :], bank[4][:, 0:SUBTILES], float(TOKENS // 2), None, ALU.add).then_inc(i_map, 1)

            dve.wait_ge(r_exp, 1)
            step(nc.vector.tensor_scalar(denom[:, :], ratio[:, :], 1.0, None, ALU.add))
            step(nc.vector.reciprocal(weight[:, 0, :], denom[:, :]))
            nc.vector.tensor_tensor(weight[:, 1, :], ratio[:, :], weight[:, 0, :], ALU.mult).then_inc(f_weight, 1)

            THIRD = 2 * HR // CR

            def weight_low(j, u, c):
                if c == 0:
                    nc.vector.tensor_copy(eb1[:, u, :], e1_sb[:, u, 2 * HR:W1_ALL])
                dve.wait_ge(e_whi, CR * j + c + 1)
                at = slice(c * THIRD, (c + 1) * THIRD)
                ins = nc.vector.tensor_tensor(e1_lo[:, u, at], e1_sb[:, u, at], e1_hi[:, u, at].bitcast(fp32), ALU.subtract)
                if c == CR - 1:
                    ins.then_inc(e_wlo, 1)

            def rows_low(j, u):
                dve.wait_ge(e_xhi, j + 1 + RING)
                nc.vector.tensor_tensor(xsT_lo[:, u, :], bank[2 + u][:, 0:SLOTS], xsT_hi[:, u, :].bitcast(fp32),
                                        ALU.subtract).then_inc(e_xlo, 1)

            def expert_rows(j, u, pair, more):
                for c in range(CR):
                    m = CR * j + c
                    g = (CR * u + c) % 2
                    dve.wait_ge(e_a, m + 1)
                    dve.wait_ge(e_gate, m + 1 + RING)
                    nc.vector.scalar_tensor_tensor(eact[:, u, c, :], bank[6 + g][:, 0:SLOTS], eb1[:, u, c:c + 1],
                                                   egate[:, g, :], ALU.add, ALU.mult).then_inc(e_act, 1)
                    if more:
                        if c == 0:
                            dve.wait_ge(e_w1[1 - u], 16 * (pair + u) + 16)
                        weight_low(j + 1, 1 - u, c)
                if more:
                    rows_low(j + 1, 1 - u)
                dve.wait_ge(e_y, j + 1 + RING)
                dve.wait_ge(e_st[u], 16 * pair + 16)
                for s in range(SUB):
                    last = nc.vector.tensor_tensor(ys_sb[:, u, s, :], bank[s][:, 0:D], eb2[:, u, :], ALU.add)
                last.then_inc(e_yev, 1)

            dve.wait_ge(e_w1[0], 16)
            for c in range(CR):
                weight_low(0, 0, c)
            rows_low(0, 0)
            with dve.Fori(0, E_PAIRS) as i:
                for u in range(2):
                    expert_rows(2 * i + u, u, i, True)
            expert_rows(EXPERT_TILES - 1, 0, E_PAIRS, False)

            def scores_out(i, k):
                u, j = k // TPB, k % TPB
                w = SEQ - j * P
                dve.wait_ge(c_s, 2 * TPB * i + k + 1)
                nc.vector.tensor_tensor(sT[:, u, j, 0:w], bank[2 + k % 2][:, 0:w], mask[:, 0:w], ALU.mult).then_inc(c_mask, 1)

            def row_stats(b, u):
                dve.wait_ge(c_o, b + 1 + RING)
                for t in range(TPB):
                    last = nc.vector.bn_stats(o_stats[:, u * TPB + t, :], bank[u][:, t * D:(t + 1) * D])
                last.then_inc(c_stat, 1)

            def shared_act(i, k):
                m = 2 * CS * i + k
                c = k % CS
                dve.wait_ge(d_a, m + 1)
                dve.wait_ge(d_gate, m + 1 + RING)
                if c == 0:
                    dve.wait_ge(d_y, 2 * i + k // CS + 1)
                nc.vector.scalar_tensor_tensor(act_sb[:, k // CS, c, :], bank[6 + k % 2][:, :], bcol[:, B_S1 + c:B_S1 + c + 1],
                                               gate_sb[:, k % 2, :], ALU.add, ALU.mult).then_inc(d_act, 1)

            def add_attention(b):
                at = ds(b * TPB, TPB)
                dve.wait_ge(c_on, b + 1 + RING)
                nc.vector.tensor_tensor(on_all[:, at, :], on_all[:, at, :],
                                        brow[:, R_LNW:R_LNW + D].unsqueeze(1).to_broadcast([P, TPB, D]), ALU.mult).then_inc(f_w, 1)
                dve.wait_ge(f_w, b + 1)
                nc.vector.tensor_tensor(acc[:, at, :], acc[:, at, :], on_all[:, at, :], ALU.add).then_inc(f_res, 1)

            def add_shared(b, u):
                at = ds(b * TPB, TPB)
                dve.wait_ge(d_y, b + 1 + RING)
                dve.wait_ge(f_res, b + 1)
                nc.vector.tensor_tensor(acc[:, at, :], acc[:, at, :], bank[2 + u][:, :].rearrange("p (t d) -> p t d", d=D),
                                        ALU.add).then_inc(d_acc, 1)

            def add_experts(b, u):
                at = ds(b * TPB, TPB)
                dve.wait_ge(f_scaled, b + 1)
                dve.wait_ge(d_acc, b + 1 + RING)
                nc.vector.tensor_tensor(acc[:, at, :], acc[:, at, :], y_st[:, u, 0, :, :], ALU.add).then_inc(f_y0, 1)
                dve.wait_ge(f_y0, b + 1)
                nc.vector.tensor_tensor(acc[:, at, :], acc[:, at, :], y_st[:, u, 1, :, :], ALU.add).then_inc(f_done, 1)

            dve.wait_ge(e_side, 2 * SIDE_PAIRS)
            with dve.Fori(0, PAIRS) as i:
                for k in range(TPB + 2):
                    scores_out(i, k)
                row_stats(2 * i, 0)
                for k in range(TPB + 2, 2 * TPB):
                    scores_out(i, k)
                row_stats(2 * i + 1, 1)
                dve.wait_ge(c_stat, 2 * i + 2)
                moments(o_stats[:, :, :], o_mean[:, :], o_var_eps[:, :], o_diff[:, :], c_step, 6 * i, c_var)
                shared_act(i, 0)
                dve.wait_ge(c_rstd, i + 1)
                nc.vector.scalar_tensor_tensor(o_shift[:, :], o_mean[:, :], -1.0, o_rstd[:, :], ALU.mult, ALU.mult).then_inc(c_shift, 1)
                for k in range(1, CS + 1):
                    shared_act(i, k)
                add_attention(2 * i)
                add_attention(2 * i + 1)
                for k in range(CS + 1, 2 * CS):
                    shared_act(i, k)
                for u in range(2):
                    add_shared(2 * i + u, u)
                for u in range(2):
                    add_experts(2 * i + u, u)

        @block.tensor
        def _(pe):
            mm = nc.tensor.matmul
            for s in (a_tr, a_lg, b_o, i_mm, e_tr, e_y, c_o, d_y):
                pe.sem_inc(s, RING)

            def split_mm(dst, w_high, w_low, x_high, x_low):
                mm(dst, w_high, x_high, start=True, stop=False)
                mm(dst, w_high, x_low, start=False, stop=False)
                return mm(dst, w_low, x_high, start=False, stop=True)

            pe.wait_ge(const_in, 16)
            pe.wait_ge(bias_in, 48)
            with pe.Fori(0, PAIRS) as i:
                for u in range(2):
                    b = 2 * i + u
                    pe.wait_ge(a_xn, b + 1 + RING)
                    pe.wait_ge(a_xn_act, b + 1)
                    pe.wait_ge(a_hi, b + 1)
                    for t in range(TPB):
                        last = nc.tensor.transpose(bank[4 + u][:, t * P:(t + 1) * P], xn_st[:, u, t, :], ident)
                    last.then_inc(a_tr, 1)
                for u in range(2):
                    b = 2 * i + u
                    pe.wait_ge(a_st, b + 1 + RING)
                    for t in range(TPB):
                        last = mm(bank[6][:, ds((b * TPB + t) * E, E)], xnT_st[:, u, t * P:(t + 1) * P], wr_sb[:, :],
                                  start=True, stop=True)
                    last.then_inc(a_lg, 1)

            def hidden(m, b, n, h):
                pe.wait_ge(b_gelu, m + 1)
                split_mm(bank[h][:, :], w1_hi[:, n * D:(n + 1) * D], w1_lo[:, n * D:(n + 1) * D],
                         xT_hi[:, ds(b * SEQ, SEQ)], xT_lo[:, ds(b * SEQ, SEQ)]).then_inc(b_h, 1)

            def second(m, n, h):
                pe.wait_ge(b_gelu, m + 1 + RING)
                pe.wait_ge(b_evac, m + 1)
                if n < 2:
                    mm(bank[2 + h][:, :], w2_sb[:, n, :], h_sb[:, h, :], start=True, stop=True).then_inc(b_o, 1)
                else:
                    for t in range(TPB):
                        last = mm(bank[2 + h][:, t * D:(t + 1) * D], h_sb[:, h, t * P:(t + 1) * P], w2_sb[:, n, :],
                                  start=True, stop=True)
                    last.then_inc(b_o, 1)

            def qkv_pair(i):
                for k in range(6):
                    hidden(6 * i + k, 2 * i + k // 3, k % 3, k % 2)
                    if k:
                        second(6 * i + k - 1, (k - 1) % 3, (k - 1) % 2)
                second(6 * i + 5, 2, 1)

            pe.wait_ge(w_low, 2)
            pe.wait_ge(a_lo, BATCH + RING)
            qkv_pair(0)
            pe.wait_ge(r_taken, 1)
            pe.wait_ge(cast, 2)
            pe.wait_ge(set_up, 4)
            mm(bank[6][:, 0:ET], before16[:, :], taken[:, :], start=True, stop=True).then_inc(r_rank, 1)
            mm(bank[7][:, 0:ET], ones16[:, :], taken[:, :], start=True, stop=True).then_inc(r_rank, 1)
            with pe.Fori(1, PAIRS) as i:
                qkv_pair(i)

            mm(bank[4][:, 0:SUBTILES], zeros16[:, :], zeros16[:, 0:SUBTILES], start=True, stop=False)
            with pe.Fori(0, INV_STEPS // 2) as i:
                for u in range(2):
                    pe.wait_ge(i_high, 2 * i + u + 1)
                    for c in range(CHUNK):
                        last = mm(bank[4][:, 0:SUBTILES], low_hot[:, u, c, :], high_token[:, u, c, :], start=False, stop=False)
                    last.then_inc(i_mm, 1)
            mm(bank[4][:, 0:SUBTILES], zeros16[:, :], zeros16[:, 0:SUBTILES], start=False, stop=True).then_inc(i_done, 1)

            def slot_transposes(j, u, pair):
                pe.wait_ge(e_x[u], 16 * SUB * pair + 16 * SUB)
                pe.wait_ge(e_xlo, j + 1)
                for s in range(SUB):
                    last = nc.tensor.transpose(bank[2 + u][:, s * P:(s + 1) * P], xs_sb[:, u, s, :], ident)
                last.then_inc(e_tr, 1)

            def expert(j, u, pair, more):
                pe.wait_ge(e_wlo, j + 1 + RING)
                pe.wait_ge(e_xlo, j + 1 + RING)
                for c in range(CR):
                    m = CR * j + c
                    g = (CR * u + c) % 2
                    pe.wait_ge(e_gate, m + 1)
                    at = slice(HR + c * P, HR + (c + 1) * P)
                    split_mm(bank[4 + g][:, 0:SLOTS], e1_hi[:, u, at], e1_lo[:, u, at], xsT_hi[:, u, :], xsT_lo[:, u, :]).then_inc(e_g, 1)
                    pe.wait_ge(e_act, m + 1)
                    at = slice(c * P, (c + 1) * P)
                    split_mm(bank[6 + g][:, 0:SLOTS], e1_hi[:, u, at], e1_lo[:, u, at], xsT_hi[:, u, :], xsT_lo[:, u, :]).then_inc(e_a, 1)
                if more:
                    slot_transposes(j + 1, 1 - u, pair + u)
                pe.wait_ge(e_w2[u], 16 * pair + 16)
                pe.wait_ge(e_yev, j + 2)
                for c in range(CR):
                    pe.wait_ge(e_act, CR * j + c + 1 + RING)
                    for s in range(SUB):
                        last = mm(bank[s][:, 0:D], eact[:, u, c, s * P:(s + 1) * P], e2_sb[:, u, c * D:(c + 1) * D],
                                  start=(c == 0), stop=(c == CR - 1))
                last.then_inc(e_y, 1)

            pe.wait_ge(b_evac, B_ITEMS + RING)
            pe.wait_ge(i_map, 1)
            slot_transposes(0, 0, 0)
            with pe.Fori(0, E_PAIRS) as i:
                for u in range(2):
                    expert(2 * i + u, u, i, True)
            expert(EXPERT_TILES - 1, 0, E_PAIRS, False)

            def scores(i, k):
                u, j = k // TPB, k % TPB
                b = 2 * i + u
                if j == 0:
                    pe.wait_ge(c_k, b + 1)
                pe.wait_ge(c_mask, 2 * TPB * i + k + 1)
                mm(bank[2 + k % 2][:, 0:SEQ - j * P], kT_st[:, u, j * P:(j + 1) * P],
                   qT_all[:, ds(b * SEQ + j * P, SEQ - j * P)], start=True, stop=True).then_inc(c_s, 1)

            def attend(i, u):
                b = 2 * i + u
                pe.wait_ge(c_mask, 2 * TPB * i + TPB * (u + 1) + RING)
                pe.wait_ge(c_on, b + 1)
                for t in range(TPB):
                    for j in range(t + 1):
                        last = mm(bank[u][:, t * D:(t + 1) * D], sT[:, u, j, (t - j) * P:(t - j + 1) * P],
                                  v_all[:, ds(b * TPB + j, 1), :].rearrange("p a d -> p (a d)"), start=(j == 0), stop=(j == t))
                last.then_inc(c_o, 1)

            def shared_up(i, k):
                m = 2 * CS * i + k
                c = k % CS
                at = ds((2 * i + k // CS) * SEQ, SEQ)
                pe.wait_ge(d_gate, m + 1)
                cols = slice(HS + c * P, HS + (c + 1) * P)
                split_mm(bank[4 + k % 2][:, :], ws1_hi[:, cols], ws1_lo[:, cols], xT_hi[:, at], xT_lo[:, at]).then_inc(d_g, 1)
                pe.wait_ge(d_act, m + 1)
                cols = slice(c * P, (c + 1) * P)
                split_mm(bank[6 + k % 2][:, :], ws1_hi[:, cols], ws1_lo[:, cols], xT_hi[:, at], xT_lo[:, at]).then_inc(d_a, 1)

            def shared_down(i, u):
                pe.wait_ge(d_act, 2 * CS * i + CS * (u + 1) + RING)
                pe.wait_ge(c_mask, 2 * TPB * (i + 1) + RING)
                for t in range(TPB):
                    for c in range(CS):
                        last = mm(bank[2 + u][:, t * D:(t + 1) * D], act_sb[:, u, c, t * P:(t + 1) * P], ws2_sb[:, c, :],
                                  start=(c == 0), stop=(c == CS - 1))
                last.then_inc(d_y, 1)

            pe.wait_ge(e_yev, EXPERT_TILES + RING)
            pe.wait_ge(e_side, 2 * SIDE_PAIRS)
            with pe.Fori(0, PAIRS) as i:
                pe.wait_ge(d_acc, 2 * i + RING)
                for k in range(TPB + 2):
                    scores(i, k)
                attend(i, 0)
                for k in range(TPB + 2, 2 * TPB):
                    scores(i, k)
                attend(i, 1)
                for k in range(CS + 1):
                    shared_up(i, k)
                shared_down(i, 0)
                for k in range(CS + 1, 2 * CS):
                    shared_up(i, k)
                shared_down(i, 1)


def kernel(**inputs):
    import numpy as np
    import concourse.bacc as bacc
    from concourse.bass_utils import run_bass_kernel_spmd

    def a(name):
        return np.ascontiguousarray(inputs["L0_" + name])

    c = np.zeros((P, C_ALL), np.float32)
    row, col = np.arange(P)[:, None], np.arange(P)[None, :]
    c[:, C_ID:C_ID + P] = row == col
    c[:, C_MASK:C_MASK + SEQ] = 1.0
    c[:, C_MASK:C_MASK + P] = col >= row
    c[:, C_BEFORE:C_BEFORE + P] = row < col
    c[:, C_REV:C_REV + ET] = np.repeat(E - np.arange(E), TILES)
    c[:, C_TILE:C_IOTA] = np.repeat(np.arange(EXPERT_TILES), E)
    c[:, C_IOTA:C_TOKEN] = col
    c[:, C_TOKEN:C_ALL] = np.tile(np.arange(TILES), TOP)[None, :] * P + row - TOKENS // 2
    cols = [a(f"attn_b1{n}") for n in "qkv"] + [a("attn_b2q"), a("attn_b2k")]
    cols = np.concatenate([np.stack(cols), a("ffn_bs1").reshape(-1, P)])
    rows = np.concatenate([a("ffn_br"), a("attn_b2v"), a("attn_ln_w"), a("attn_ln_b"), a("ffn_bs2")])
    be1 = a("ffn_be1").reshape(E, 2 * CR, P).transpose(0, 2, 1)
    we2 = a("ffn_We2").reshape(E, CR, P, D).transpose(0, 2, 1, 3).reshape(E, P, CR * D)
    be2 = np.broadcast_to(a("ffn_be2")[:, None, :], (E, P, D))
    arrays = {
        "x": a("attn_x"), "w1": np.stack([a(f"attn_W1{n}") for n in "qkv"]), "w2": np.stack([a(f"attn_W2{n}") for n in "qkv"]),
        "ws1": a("ffn_Ws1"), "ws2": a("ffn_Ws2"), "expert1": np.concatenate([a("ffn_We1"), be1], axis=2),
        "expert2": np.concatenate([we2, be2], axis=2), "wr": a("ffn_Wr"), "consts": c,
        "bias_cols": np.ascontiguousarray(cols.T), "bias_rows": np.ascontiguousarray(np.broadcast_to(rows[None, :], (P, rows.size))),
    }
    nc = bacc.Bacc("TRN2", target_bir_lowering=False, num_devices=1)
    args = [nc.dram_tensor(f"in_{n}", v.shape, mybir.dt.from_np(v.dtype), kind="ExternalInput").ap() for n, v in arrays.items()]
    out = nc.dram_tensor("out_0", (BATCH, SEQ, D), mybir.dt.float32, kind="ExternalOutput").ap()
    block_kernel(nc, *args, out)
    r = run_bass_kernel_spmd(nc, [{f"in_{n}": v for n, v in arrays.items()}], core_ids=[0])
    return r.results[0]["out_0"]
```

```python
import concourse.bass as bass
from concourse import mybir
from contextlib import ExitStack

P = 128
BATCH, SEQ, D = 8, 512, 128
TOKENS = BATCH * SEQ
TPB = SEQ // P
TILES = TOKENS // P
E, TOP = 12, 2
HS, HR = 2 * D, 3 * D
CS, CR = HS // P, HR // P
SLOTS = 256
SUB = SLOTS // P
EXPERT_TILES = (TOP * TOKENS + E * (SLOTS - 1)) // SLOTS
ALL_SLOTS = EXPERT_TILES * SLOTS
SUBTILES = ALL_SLOTS // P
EPS = 1e-5
INV_SCALE = 1.0 / float(128 * 256) ** 0.5
INV_TAU = 1.0 / 1.5
MASKED = -3.0e38
ASSIGN = TOP * TILES
ET = E * TILES

PAIRS = BATCH // 2
E_PAIRS = EXPERT_TILES // 2
CHUNK = 8
WARM, KEEP_WARM = 48, 12
POOL_ROWS = 3
INV_RING = 4
INV_STEPS = ASSIGN // CHUNK
RING = 2
WEIGHT_RING = 4
E_TURNS = (EXPERT_TILES - 2) // WEIGHT_RING

C_ID = 0
C_MASK = C_ID + P
C_BEFORE = C_MASK + SEQ
C_REV = C_BEFORE + P
C_TILE = C_REV + ET
C_IOTA = C_TILE + EXPERT_TILES * E
C_TOKEN = C_IOTA + P
C_ALL = C_TOKEN + ASSIGN

B_1 = 0
B_2 = 3
B_S1 = 5
B_ALL = B_S1 + 2 * CS

R_BR = 0
R_B2V = R_BR + E
R_LNW = R_B2V + D
R_LNB = R_LNW + D
R_BS2 = R_LNB + D
R_ALL = R_BS2 + D

W1_ALL = 2 * HR + 2 * CR
W2_ALL = CR * D + D


def block_kernel(nc, x, w1, w2, ws1, ws2, expert1, expert2, wr, consts, bias_cols, bias_rows, out):
    fp32, fp32r, fp16 = mybir.dt.float32, mybir.dt.float32r, mybir.dt.float16
    i32, u32 = mybir.dt.int32, mybir.dt.uint32
    ALU, ACT, AX = mybir.AluOpType, mybir.ActivationFunctionType, mybir.AxisListType
    ds = bass.ds

    x_tiled = x.rearrange("b (t p) d -> p (b t) d", p=P)
    out_tiled = out.rearrange("b (t p) d -> p (b t) d", p=P)
    xn_rows = nc.dram_tensor("xn_rows", [TOKENS, D], fp32, kind="Internal").ap()
    slot_y = nc.dram_tensor("slot_y", [ALL_SLOTS, D], fp32, kind="Internal").ap()
    xn_tiled = xn_rows.rearrange("(t p) d -> p t d", p=P)
    slot_y_tiled = slot_y.rearrange("(t p) d -> p t d", p=P)
    expert1_rows = expert1.rearrange("e p h -> (e p) h")
    expert2_rows = expert2.rearrange("e p h -> (e p) h")

    ctx = ExitStack()
    with ctx:
        def sb(name, shape, dt=fp32):
            return ctx.enter_context(nc.sbuf_tensor(name, shape, dt))

        def sem(name):
            return ctx.enter_context(nc.semaphore(name))

        def sems(*names):
            return [sem(n) for n in names]

        x_all = sb("x_all", [P, TILES, D])
        xT_hi, xT_lo = sb("xT_hi", [P, TOKENS], fp32r), sb("xT_lo", [P, TOKENS], fp32r)
        qT_all = sb("qT_all", [P, TOKENS])
        kT_all = sb("kT_all", [P, TOKENS])
        v_all = sb("v_all", [P, TILES, D])
        acc = sb("acc", [P, TILES, D])
        on_all = x_all

        w1_sb = sb("w1_sb", [P, 3 * D])
        w1_hi, w1_lo = sb("w1_hi", [P, 3 * D], fp32r), sb("w1_lo", [P, 3 * D], fp32r)
        w2_sb = sb("w2_sb", [P, 3, D])
        ws1_sb = sb("ws1_sb", [P, 2 * HS])
        ws1_hi, ws1_lo = sb("ws1_hi", [P, 2 * HS], fp32r), sb("ws1_lo", [P, 2 * HS], fp32r)
        ws2_sb = sb("ws2_sb", [P, CS, D])
        wr_sb = sb("wr_sb", [P, E])
        cst = sb("cst", [P, C_ALL])
        bcol = sb("bcol", [P, B_ALL])
        brow = sb("brow", [P, R_ALL])
        ident = cst[:, C_ID:C_ID + P]
        mask = cst[:, C_MASK:C_MASK + SEQ]
        rev = cst[:, C_REV:C_REV + ET]
        tile_no = cst[:, C_TILE:C_TILE + EXPERT_TILES * E]
        token = cst[:, C_TOKEN:C_TOKEN + ASSIGN]
        before16, ones16, zeros16, iota16 = (sb(n, [P, P], fp16) for n in ("before16", "ones16", "zeros16", "iota16"))
        qbias = sb("qbias", [P, 1])
        lnb_bs2 = sb("lnb_bs2", [P, D])
        half_neg = sb("half_neg", [P, TILES])
        table_in = sb("table_in", [P, 1])

        x_stats = sb("x_stats", [P, TILES, 6])
        x_mean, x_rstd, x_shift = (sb(n, [P, TILES]) for n in ("x_mean", "x_rstd", "x_shift"))
        var_eps, diff = sb("var_eps", [P, TILES]), sb("diff", [P, TILES])
        xn_all = acc

        scratch = sb("scratch", [P, 9 * ET])
        lg, lg2, hit, total, cum, pos, ones_et = (scratch[:, n * ET:(n + 1) * ET] for n in range(7))
        picked = scratch[:, 1 * ET:3 * ET].rearrange("p (k n) -> p k n", k=TOP)
        best = sb("best", [P, TOP, TILES])
        first = sb("first", [P, TILES])
        choice = scratch[:, 7 * ET:9 * ET].rearrange("p (k n) -> p k n", k=TOP)
        taken = sb("taken", [P, ET], fp16)
        cnt_f, tiles_f, tile_end, run_off = (sb(n, [P, E]) for n in ("cnt_f", "tiles_f", "tile_end", "run_off"))
        cnt_i, tiles_i = sb("cnt_i", [P, E], i32), sb("tiles_i", [P, E], i32)
        slot_f = sb("slot_f", [P, TOP, TILES])
        slot = sb("slot", [P, TOP, TILES], u32)
        ended = scratch[:, 2 * W1_ALL:2 * W1_ALL + EXPERT_TILES * E]
        owner_f = sb("owner_f", [P, EXPERT_TILES])
        owner = sb("owner", [P, EXPERT_TILES], i32)
        gap, ratio, denom = (sb(n, [P, TILES]) for n in ("gap", "ratio", "denom"))
        weight = sb("weight", [P, TOP, TILES])

        h_sb = sb("h_sb", [P, 2, SEQ])
        kT_st = h_sb
        gate_sb = sb("gate_sb", [P, 2, SEQ])
        sT = sb("sT", [P, 2, TPB, SEQ])
        xnT = [sT[:, b // TPB, b % TPB, :] for b in range(BATCH)]
        act_sb = sT[:, 1, :, :].rearrange("p (u c) s -> p u c s", u=2)
        eact = sT[:, 0, 0:CR, :].rearrange("p c (u s) -> p u c s", u=2)

        slot_i, high_i, low_i = (sb(n, [P, ASSIGN], i32) for n in ("slot_i", "high_i", "low_i"))
        high, low16 = sb("high", [P, ASSIGN]), sb("low16", [P, ASSIGN], fp16)
        high_st, token_st = sb("high_st", [P, INV_RING, CHUNK]), sb("token_st", [P, INV_RING, CHUNK])
        low_hot = sT[:, 0, :, :].rearrange("p t s -> p (t s)").bitcast(fp16).rearrange(
            "p (n r) -> p n r", r=P)[:, 0:INV_RING * CHUNK, :].rearrange("p (u c) r -> p u c r", u=INV_RING)
        high_token = sT[:, 1, :, :].rearrange("p t s -> p (t s)").bitcast(fp16)[:, 0:INV_RING * CHUNK * SUBTILES].rearrange(
            "p (u c a) -> p u c a", u=INV_RING, a=SUBTILES)
        slot_token = sb("slot_token", [P, SUBTILES], u32)

        spare = sT[:, 1, :, :].rearrange("p t s -> p (t s)")
        e1_sb = [scratch[:, 0:W1_ALL], scratch[:, W1_ALL:2 * W1_ALL], spare[:, 2 * W2_ALL:2 * W2_ALL + W1_ALL],
                 cst[:, C_BEFORE:C_BEFORE + W1_ALL]]
        e1_hi, e1_lo = sb("e1_hi", [P, 2, 2 * HR], fp32r), sb("e1_lo", [P, 2, 2 * HR], fp32r)
        eb1 = sb("eb1", [P, 2, 2 * CR])
        e2_first = sb("e2_first", [P, 2, W2_ALL])
        e2_sb = [e2_first[:, 0, :], e2_first[:, 1, :], spare[:, 0:W2_ALL], spare[:, W2_ALL:2 * W2_ALL]]
        idx_st = sb("idx_st", [P, 2, SUB], u32)
        xs_sb = sb("xs_sb", [P, 2, SUB, D])
        xsT_hi, xsT_lo = sb("xsT_hi", [P, 2, SLOTS], fp32r), sb("xsT_lo", [P, 2, SLOTS], fp32r)
        egate = gate_sb[:, :, 0:SLOTS]
        ys_sb = sb("ys_sb", [P, 2, SUB, D])
        o_stats = sb("o_stats", [P, 2 * TPB, 6])
        o_mean, o_rstd, o_shift, o_var_eps, o_diff, o_prod = (sb(n, [P, 2 * TPB]) for n in ("o_mean", "o_rstd", "o_shift", "o_var_eps", "o_diff", "o_prod"))
        o_bits = sb("o_bits", [P, 2 * TPB], i32)
        y_st = scratch[:, 0:2 * TOP * SEQ].rearrange("p (u k t d) -> p u k t d", u=2, k=TOP, d=D)

        bank = [ctx.enter_context(nc.psum_tensor(f"bank{i}", [P, 512], fp32)) for i in range(8)]

        ident_in, const_in, bias_in, w1_in, w_in = sems("ident_in", "const_in", "bias_in", "w1_in", "w_in")
        x_in = [sem(f"x_in{q}") for q in range(4)]
        set_up, cast, w_high, w_low = sems("set_up", "cast", "w_high", "w_low")
        a_stat, a_step, a_var, a_rstd, a_shift = sems("a_stat", "a_step", "a_var", "a_rstd", "a_shift")
        a_xn, a_xn_act, a_tr, a_st, a_hi, a_lo, a_lg = sems("a_xn", "a_xn_act", "a_tr", "a_st", "a_hi", "a_lo", "a_lg")
        kept = sem("kept")
        b_h, b_gelu, b_o, b_evac = sems("b_h", "b_gelu", "b_o", "b_evac")
        r_step, r_taken, r_rank, r_slot, r_split, r_owner, r_gap, r_exp = sems(
            "r_step", "r_taken", "r_rank", "r_slot", "r_split", "r_owner", "r_gap", "r_exp")
        i_st, i_high, i_pool, i_mm, i_map = sems("i_st", "i_high", "i_pool", "i_mm", "i_map")
        e_x, e_st = (sems(f"{n}0", f"{n}1") for n in ("e_x", "e_st"))
        e_w1, e_w2 = ([sem(f"{n}{k}") for k in range(WEIGHT_RING)] for n in ("e_w1", "e_w2"))
        e_idx, e_tr, e_xhi, e_xlo, e_whi, e_wlo = sems("e_idx", "e_tr", "e_xhi", "e_xlo", "e_whi", "e_wlo")
        e_g, e_a, e_gate, e_act, e_y, e_yev = sems("e_g", "e_a", "e_gate", "e_act", "e_y", "e_yev")
        e_side, wait_holder = sems("e_side", "wait_holder")
        c_k, c_s, c_mask, c_o, c_stat, c_step, c_var, c_root, c_shift, c_on = sems(
            "c_k", "c_s", "c_mask", "c_o", "c_stat", "c_step", "c_var", "c_root", "c_shift", "c_on")
        d_g, d_a, d_gate, d_act, d_y, d_acc = sems("d_g", "d_a", "d_gate", "d_act", "d_y", "d_acc")
        gathered = [sems(f"gathered{u}0", f"gathered{u}1") for u in range(2)]
        f_weight, f_scaled, f_w, f_y0, f_y1, f_res, stored = sems(
            "f_weight", "f_scaled", "f_w", "f_y0", "f_y1", "f_res", "stored")

        B_ITEMS, D_ITEMS = 3 * BATCH, CS * BATCH
        def expert_tile(i, n):
            return WEIGHT_RING * i + n, n % WEIGHT_RING, i + n // WEIGHT_RING, WEIGHT_RING // 2 * i + n // 2

        ROOT_STEPS = 11
        HIDDEN_BANKS = (0, 1, 5)
        SCORE_BANKS = (2, 3, 6, 7)
        SIDE_PAIRS = TILES // 2
        QT = TILES // 4
        HALF = TILES // 2

        block = ctx.enter_context(nc.Block())

        @block.sync
        def _(sp):
            for s in e_st:
                sp.sem_inc(s, 16)
            for q in range(4):
                sp.dma_start(x_all[:, q * QT:(q + 1) * QT, :], x_tiled[:, q * QT:(q + 1) * QT, :]).then_inc(x_in[q], 16)
                if q == 1:
                    sp.dma_start(cst[:, 0:C_MASK], consts[:, 0:C_MASK]).then_inc(ident_in, 16)
                    sp.dma_start(wr_sb[:, :], wr).then_inc(ident_in, 16)
            sp.dma_start(cst[:, C_MASK:C_ALL], consts[:, C_MASK:C_ALL]).then_inc(const_in, 16)
            sp.dma_start(brow[:, :], bias_rows).then_inc(bias_in, 16)
            sp.dma_start(bcol[:, :], bias_cols).then_inc(bias_in, 16)
            for n in range(3):
                sp.dma_start(w1_sb[:, n * D:(n + 1) * D], w1[n]).then_inc(w1_in, 16)
            for n in range(3):
                sp.dma_start(w2_sb[:, n, :], w2[n]).then_inc(w_in, 16)
            sp.dma_start(ws1_sb[:, :], ws1).then_inc(w_in, 16)
            sp.dma_start(ws2_sb[:, :, :], ws2.rearrange("(c p) d -> p c d", p=P)).then_inc(w_in, 16)
            for q in range(4):
                sp.wait_ge(a_xn, 2 * q + 2)
                sp.wait_ge(a_xn_act, 2 * q + 2)
                sp.dma_start(xn_tiled[:, q * QT:(q + 1) * QT, :], xn_all[:, q * QT:(q + 1) * QT, :]).then_inc(kept, 16)

            def owner_rows(j):
                return ds(sp.value_load(owner[0:1, ds(j, 1)], min_val=0, max_val=E - 1) * P, P)

            def load_first(t):
                j, k, _, _ = t
                rows = owner_rows(j)
                if not (isinstance(j, int) and j < WEIGHT_RING):
                    sp.wait_ge(e_wlo, CR * (j - 1))
                    sp.sem_inc(wait_holder, 1)
                sp.dma_start(e1_sb[k], expert1_rows[rows, :]).then_inc(e_w1[k], 16)

            def load_second(t):
                j, k, _, _ = t
                rows = owner_rows(j)
                if not (isinstance(j, int) and j < WEIGHT_RING):
                    sp.wait_ge(e_yev, j - 1)
                    sp.sem_inc(wait_holder, 1)
                sp.dma_start(e2_sb[k], expert2_rows[rows, :]).then_inc(e_w2[k], 16)

            def store(t):
                j, k, _, _ = t
                sp.wait_ge(e_yev, j + 1 + RING)
                sp.dma_start(slot_y_tiled[:, ds(j * SUB, SUB), :], ys_sb[:, k % 2, :, :]).then_inc(e_st[k % 2], 16)

            sp.wait_ge(r_owner, 1)
            sp.wait_ge(r_slot, 1)
            for n in range(2):
                load_first(expert_tile(0, n))
            for n in range(2):
                load_second(expert_tile(0, n))
            sp.wait_ge(i_map, 1)
            sp.wait_ge(e_x[0], 16 * SUB)
            for n in range(2, WEIGHT_RING):
                load_first(expert_tile(0, n))
                load_second(expert_tile(0, n))
            TURNS = (EXPERT_TILES - WEIGHT_RING) // WEIGHT_RING
            with sp.Fori(0, TURNS) as i:
                for n in range(WEIGHT_RING):
                    load_first(expert_tile(i, n + WEIGHT_RING))
                    store(expert_tile(i, n))
                    load_second(expert_tile(i, n + WEIGHT_RING))
            for n in range(WEIGHT_RING * TURNS, EXPERT_TILES):
                if n + WEIGHT_RING < EXPERT_TILES:
                    load_first(expert_tile(0, n + WEIGHT_RING))
                    load_second(expert_tile(0, n + WEIGHT_RING))
                store(expert_tile(0, n))

            def store_sums(b):
                sp.dma_start(out_tiled[:, ds(b * TPB, TPB), :], acc[:, ds(b * TPB, TPB), :]).then_inc(stored, 16)

            with sp.Fori(0, BATCH) as b:
                sp.wait_ge(f_res, b + 1)
                store_sums(b)
            sp.wait_ge(stored, 16 * BATCH)

        @block.gpsimd
        def _(pool):
            nc.gpsimd.memset(half_neg[:, :], -0.5).then_inc(set_up, 1)
            nc.gpsimd.memset(ones16[:, :], 1.0).then_inc(set_up, 1)
            nc.gpsimd.memset(zeros16[:, :], 0.0).then_inc(set_up, 1)
            nc.gpsimd.memset(ones_et[:, :], 1.0).then_inc(set_up, 1)
            pool.wait_ge(set_up, 4)

            def a_root(q):
                at = slice(q * QT, (q + 1) * QT)
                pool.wait_ge(a_var, q + 1)
                nc.gpsimd.tensor_tensor(x_rstd[:, at], var_eps[:, at], half_neg[:, at], ALU.pow).then_inc(a_rstd, 1)

            def a_low(b):
                pool.wait_ge(a_hi, b + 1)
                at = slice(b * SEQ, (b + 1) * SEQ)
                nc.gpsimd.tensor_tensor(xT_lo[:, at], xnT[b], xT_hi[:, at].bitcast(fp32), ALU.subtract).then_inc(a_lo, 1)

            a_root(0)
            a_root(1)
            a_low(0)
            a_root(2)
            a_low(1)
            a_root(3)
            for b in range(2, BATCH - 2):
                a_low(b)
            pool.wait_ge(w_high, 1)
            nc.gpsimd.tensor_tensor(w1_lo[:, :], w1_sb[:, :], w1_hi[:, :].bitcast(fp32), ALU.subtract).then_inc(w_low, 1)
            for b in range(BATCH - 2, BATCH):
                a_low(b)
            pool.wait_ge(w_high, 3)
            nc.gpsimd.tensor_tensor(ws1_lo[:, :], ws1_sb[:, :], ws1_hi[:, :].bitcast(fp32), ALU.subtract).then_inc(w_low, 1)

            with pool.Fori(0, INV_STEPS // INV_RING) as i:
                for u in range(INV_RING):
                    q = INV_RING * i + u
                    pool.wait_ge(i_st, 2 * q + 2)
                    pool.sem_inc(wait_holder, 1)
                    for c in range(POOL_ROWS):
                        last = nc.gpsimd.tensor_scalar(high_token[:, u, c, :], iota16[:, 0:SUBTILES], high_st[:, u, c:c + 1],
                                                       token_st[:, u, c:c + 1], ALU.is_equal, ALU.mult)
                    last.then_inc(i_pool, 1)

            def gather_rows(j, u):
                pool.wait_ge(e_tr, j + 1)
                nc.gpsimd.tensor_copy(idx_st[:, u, :], slot_token[:, ds(j * SUB, SUB)]).then_inc(e_idx, 1)
                pool.wait_ge(e_idx, j + 1)
                pool.sem_inc(wait_holder, 1)
                for s in range(SUB):
                    nc.gpsimd.indirect_dma_start(xs_sb[:, u, s, :], None, xn_rows,
                                                 bass.IndirectOffsetOnAxis(ap=idx_st[:, u, s:s + 1], axis=0)).then_inc(e_x[u], 16)

            def prepare(i):
                at = ds(2 * i, 2)
                nc.gpsimd.tensor_tensor(acc[:, at, :], x_all[:, at, :], lnb_bs2[:, :].unsqueeze(1).to_broadcast([P, 2, D]),
                                        ALU.add).then_inc(e_side, 1)
                nc.gpsimd.tensor_tensor(v_all[:, at, :], v_all[:, at, :],
                                        brow[:, R_B2V:R_B2V + D].unsqueeze(1).to_broadcast([P, 2, D]), ALU.add).then_inc(e_side, 1)

            pool.wait_ge(i_map, 1)
            pool.wait_ge(kept, 16 * 4)
            with pool.Fori(0, SIDE_PAIRS) as i:
                for u in range(2):
                    gather_rows(2 * i + u, u)
                pool.wait_ge(b_evac, B_ITEMS + RING)
                prepare(i)
            with pool.Fori(SIDE_PAIRS, E_PAIRS) as i:
                for u in range(2):
                    gather_rows(2 * i + u, u)
            gather_rows(EXPERT_TILES - 1, 0)

            pool.wait_ge(e_st[0], 16 * (EXPERT_TILES - E_PAIRS) + 16)
            pool.wait_ge(e_st[1], 16 * E_PAIRS + 16)
            for b in range(BATCH):
                for k in range(TOP):
                    if b >= 2:
                        pool.wait_ge((f_y0, f_y1)[k], b - 1)
                    for t in range(TPB):
                        nc.gpsimd.indirect_dma_start(y_st[:, b % 2, k, t, :], None, slot_y,
                                                     bass.IndirectOffsetOnAxis(ap=slot[:, k, b * TPB + t:b * TPB + t + 1], axis=0)
                                                     ).then_inc(gathered[b % 2][k], 16)

        @block.scalar
        def _(act):
            for s in (b_gelu, b_evac, e_xhi, e_gate, c_on, d_gate):
                act.sem_inc(s, RING)

            act.wait_ge(set_up, 4)

            def a_normal(b):
                t = b * TPB + TPB - 1
                act.wait_ge(a_shift, t // QT + 1)
                nc.scalar.activation(xn_all[:, t, :], x_all[:, t, :], ACT.Identity, bias=x_shift[:, t:t + 1],
                                     scale=x_rstd[:, t:t + 1]).then_inc(a_xn_act, 1)

            def a_out(b):
                act.wait_ge(a_tr, b + 1)
                nc.scalar.activation(xnT[b], bank[4 + b % 2][:, :], ACT.Copy).then_inc(a_st, 1)
                nc.scalar.activation(xT_hi[:, b * SEQ:(b + 1) * SEQ], bank[4 + b % 2][:, :], ACT.Copy).then_inc(a_hi, 1)

            nc.scalar.activation(table_in[:, :], half_neg[:, 0:1], ACT.Gelu)
            for b in range(0, BATCH, 2):
                a_normal(b)
                a_normal(b + 1)
                a_out(b)
                if b == BATCH - 4:
                    act.wait_ge(w1_in, 16 * 3)
                    nc.scalar.activation(w1_hi[:, :], w1_sb[:, :], ACT.Copy).then_inc(w_high, 1)
                a_out(b + 1)
            act.wait_ge(bias_in, 32)
            nc.scalar.mul(qbias[:, :], bcol[:, B_2:B_2 + 1], INV_SCALE).then_inc(w_high, 1)
            act.wait_ge(w_in, 16 * 5)
            nc.scalar.activation(ws1_hi[:, :], ws1_sb[:, :], ACT.Copy).then_inc(w_high, 1)
            act.wait_ge(w_high, 3)

            def gelu(m, n, h):
                act.wait_ge(b_h, m + 1)
                act.wait_ge(b_o, m + 1)
                nc.scalar.activation(h_sb[:, h, :], bank[HIDDEN_BANKS[n]][:, :], ACT.Gelu, bias=bcol[:, B_1 + n:B_1 + n + 1]).then_inc(b_gelu, 1)

            def evac(m, b, n, h):
                act.wait_ge(b_o, m + 1 + RING)
                if n == 0:
                    nc.scalar.activation(qT_all[:, ds(b * SEQ, SEQ)], bank[2 + h][:, :], ACT.Identity,
                                         bias=qbias[:, :], scale=INV_SCALE).then_inc(b_evac, 1)
                elif n == 1:
                    nc.scalar.activation(kT_all[:, ds(b * SEQ, SEQ)], bank[2 + h][:, :], ACT.Identity,
                                         bias=bcol[:, B_2 + 1:B_2 + 2]).then_inc(b_evac, 1)
                else:
                    nc.scalar.activation(v_all[:, ds(b * TPB, TPB), :],
                                         bank[2 + h][:, :].rearrange("p (t d) -> p t d", d=D), ACT.Copy).then_inc(b_evac, 1)

            def weight_high(t, c):
                j, k, use, _ = t
                if c == 0:
                    act.wait_ge(e_w1[k], 16 * use + 16)
                at = slice(c * 2 * P, (c + 1) * 2 * P)
                nc.scalar.activation(e1_hi[:, k % 2, at], e1_sb[k][:, at], ACT.Copy).then_inc(e_whi, 1)

            def rows_high(t):
                j, u = t[0], t[1] % 2
                act.wait_ge(e_tr, j + 1 + RING)
                nc.scalar.activation(xsT_hi[:, u, :], bank[2 + u][:, 0:SLOTS], ACT.Copy).then_inc(e_xhi, 1)

            def expert_gates(t, after):
                j, u = t[0], t[1] % 2
                for c in range(CR):
                    m = CR * j + c
                    g = (CR * u + c) % 2
                    act.wait_ge(e_g, m + 1)
                    act.wait_ge(e_act, m + 1)
                    nc.scalar.activation(egate[:, g, :], bank[4 + g][:, 0:SLOTS], ACT.Gelu,
                                         bias=eb1[:, u, CR + c:CR + c + 1]).then_inc(e_gate, 1)
                    if after:
                        if c == 1:
                            rows_high(after)
                        weight_high(after, c)

            def qkv_pair(i, first=False, last=False):
                for k in range(6):
                    gelu(6 * i + k, k % 3, k % 2)
                    if k:
                        evac(6 * i + k - 1, 2 * i + (k - 1) // 3, (k - 1) % 3, (k - 1) % 2)
                    elif not first:
                        evac(6 * i - 1, 2 * i - 1, 2, 1)
                    if last and 1 <= k <= CR:
                        weight_high(expert_tile(0, 0), k - 1)

            qkv_pair(0, first=True)
            with act.Fori(1, PAIRS - 1) as i:
                qkv_pair(i)
            qkv_pair(PAIRS - 1, last=True)
            evac(B_ITEMS - 1, BATCH - 1, 2, 1)

            rows_high(expert_tile(0, 0))
            expert_gates(expert_tile(0, 0), expert_tile(0, 1))
            with act.Fori(0, E_TURNS) as i:
                for n in range(1, 1 + WEIGHT_RING):
                    expert_gates(expert_tile(i, n), expert_tile(i, n + 1))
            for n in range(1 + WEIGHT_RING * E_TURNS, EXPERT_TILES):
                expert_gates(expert_tile(0, n), expert_tile(0, n + 1) if n + 1 < EXPERT_TILES else None)

            def scale_rows(b, u, turn, k):
                act.wait_ge(gathered[u][k], 16 * TPB * turn + 16 * TPB)
                for t in range(TPB):
                    last = nc.scalar.activation(y_st[:, u, k, t, :], y_st[:, u, k, t, :], ACT.Copy,
                                                scale=weight[:, k, ds(b * TPB + t, 1)])
                last.then_inc(f_scaled, 1)

            def keys(b, u):
                act.wait_ge(c_o, b + 1)
                nc.scalar.activation(kT_st[:, u, :], kT_all[:, ds(b * SEQ, SEQ)], ACT.Copy).then_inc(c_k, 1)

            def shared_gate(i, k):
                m = 2 * CS * i + k
                c = k % CS
                act.wait_ge(d_g, m + 1)
                act.wait_ge(d_act, m + 1)
                nc.scalar.activation(gate_sb[:, k % 2, :], bank[4 + k % 2][:, :], ACT.Gelu,
                                     bias=bcol[:, B_S1 + CS + c:B_S1 + CS + c + 1]).then_inc(d_gate, 1)

            def attention_rows(i, u):
                act.wait_ge(c_shift, i + 1)
                for t in range(TPB):
                    s = u * TPB + t
                    last = nc.scalar.activation(on_all[:, ds((2 * i + u) * TPB + t, 1), :].rearrange("p a d -> p (a d)"),
                                                bank[u][:, t * D:(t + 1) * D], ACT.Identity,
                                                bias=o_shift[:, s:s + 1], scale=o_rstd[:, s:s + 1])
                last.then_inc(c_on, 1)

            def tail_turn(i, first, last):
                if not first:
                    for k in range(TOP):
                        scale_rows(2 * i - 1, 1, i - 1, k)
                shared_gate(i, 0)
                if not last:
                    keys(2 * i + 2, 0)
                    keys(2 * i + 3, 1)
                shared_gate(i, 1)
                scale_rows(2 * i, 0, i, 0)
                shared_gate(i, 2)
                scale_rows(2 * i, 0, i, 1)
                shared_gate(i, 3)
                if last:
                    for k in range(TOP):
                        scale_rows(BATCH - 1, 1, PAIRS - 1, k)
                attention_rows(i, 0)
                attention_rows(i, 1)

            keys(0, 0)
            keys(1, 1)
            act.wait_ge(r_gap, 1)
            nc.scalar.activation(ratio[:, :], gap[:, :], ACT.Exp, scale=INV_TAU).then_inc(r_exp, 1)
            nc.scalar.activation(table_in[:, :], bcol[:, 0:1], ACT.Gelu)
            act.wait_ge(e_side, 2 * SIDE_PAIRS)
            act.wait_ge(f_weight, 1)
            tail_turn(0, True, False)
            with act.Fori(1, PAIRS - 1) as i:
                tail_turn(i, False, False)
            tail_turn(PAIRS - 1, False, True)

        @block.vector
        def _(dve):
            steps = [0]

            def step(ins):
                steps[0] += 1
                ins.then_inc(r_step, 1)
                dve.wait_ge(r_step, steps[0])

            def moments(stats, mean, var, dif, counter, base, made):
                even, odd = stats[:, :, 1], stats[:, :, 4]
                nc.vector.tensor_tensor(mean, even, odd, ALU.add).then_inc(counter, 1)
                nc.vector.tensor_tensor(dif, even, odd, ALU.subtract).then_inc(counter, 1)
                nc.vector.tensor_tensor(var, stats[:, :, 2], stats[:, :, 5], ALU.add).then_inc(counter, 1)
                dve.wait_ge(counter, base + 3)
                nc.vector.tensor_tensor(dif, dif, dif, ALU.mult).then_inc(counter, 1)
                nc.vector.tensor_scalar(var, var, 1.0 / D, EPS, ALU.mult, ALU.add).then_inc(counter, 1)
                nc.vector.tensor_scalar(mean, mean, 0.5, None, ALU.mult).then_inc(counter, 1)
                dve.wait_ge(counter, base + 6)
                nc.vector.scalar_tensor_tensor(var, dif, 0.25, var, ALU.mult, ALU.add).then_inc(made, 1)

            for s in (e_act, e_xlo, e_yev, c_mask, d_act, d_acc):
                dve.sem_inc(s, RING)
            dve.sem_inc(e_wlo, RING * CR)

            def a_stats(q):
                dve.wait_ge(x_in[q], 16)
                for t in range(q * QT, (q + 1) * QT):
                    last = nc.vector.bn_stats(x_stats[:, t, :], x_all[:, t, :])
                last.then_inc(a_stat, 1)
                dve.wait_ge(a_stat, q + 1)
                at = slice(q * QT, (q + 1) * QT)
                moments(x_stats[:, at, :], x_mean[:, at], var_eps[:, at], diff[:, at], a_step, 6 * q, a_var)

            def a_normal(q):
                at = slice(q * QT, (q + 1) * QT)
                dve.wait_ge(a_rstd, q + 1)
                nc.vector.scalar_tensor_tensor(x_shift[:, at], x_mean[:, at], -1.0, x_rstd[:, at], ALU.mult, ALU.mult).then_inc(a_shift, 1)
                for b in (2 * q, 2 * q + 1):
                    for t in range(b * TPB, (b + 1) * TPB - 1):
                        last = nc.vector.tensor_scalar(xn_all[:, t, :], x_all[:, t, :], x_mean[:, t:t + 1], x_rstd[:, t:t + 1],
                                                       ALU.subtract, ALU.mult)
                    last.then_inc(a_xn, 1)

            a_stats(0)
            a_stats(1)
            a_normal(0)
            a_stats(2)
            a_normal(1)
            a_stats(3)
            a_normal(2)
            a_normal(3)
            dve.wait_ge(const_in, 16)
            dve.wait_ge(bias_in, 32)
            nc.vector.tensor_copy(before16[:, :], cst[:, C_BEFORE:C_BEFORE + P]).then_inc(cast, 1)
            nc.vector.tensor_copy(iota16[:, :], cst[:, C_IOTA:C_IOTA + P]).then_inc(cast, 1)
            nc.vector.tensor_tensor(lnb_bs2[:, :], brow[:, R_LNB:R_LNB + D], brow[:, R_BS2:R_BS2 + D], ALU.add).then_inc(cast, 1)

            def et(ap):
                return ap.rearrange("p (e t) -> p e t", t=TILES)

            def te(ap):
                return ap.rearrange("p (e t) -> p t e", t=TILES)

            def over_e(ap):
                return ap.unsqueeze(1).to_broadcast([P, E, TILES])

            def over_t(ap):
                return ap.unsqueeze(2).to_broadcast([P, E, TILES])

            dve.wait_ge(a_lg, BATCH)
            step(nc.vector.tensor_tensor(et(lg[:, :]), bank[6][:, 0:ET].rearrange("p (t e) -> p e t", e=E),
                                         over_t(brow[:, R_BR:R_BR + E]), ALU.add))
            src = lg
            for k in range(TOP):
                step(nc.vector.tensor_reduce(best[:, k, :], te(src[:, :]), AX.X, ALU.max))
                step(nc.vector.tensor_tensor(et(hit[:, :]), et(src[:, :]), over_e(best[:, k, :]), ALU.is_equal))
                step(nc.vector.tensor_tensor(hit[:, :], hit[:, :], rev, ALU.mult))
                step(nc.vector.tensor_reduce(first[:, :], te(hit[:, :]), AX.X, ALU.max))
                step(nc.vector.tensor_tensor(et(choice[:, k, :]), et(rev), over_e(first[:, :]), ALU.is_equal))
                if k == 0:
                    step(nc.vector.scalar_tensor_tensor(lg2[:, :], choice[:, 0, :], MASKED, lg[:, :], ALU.mult, ALU.add))
                    src = lg2
            nc.vector.tensor_tensor(taken[:, :], choice[:, 0, :], choice[:, 1, :], ALU.add).then_inc(r_taken, 1)
            nc.vector.tensor_tensor(gap[:, :], best[:, 1, :], best[:, 0, :], ALU.subtract).then_inc(r_gap, 1)
            dve.wait_ge(set_up, 4)
            dve.wait_ge(r_rank, 2)
            step(nc.vector.tensor_tensor_scan(cum[:, :], ones_et[:, :], bank[7][:, 0:ET], 0.0, ALU.mult, ALU.add))
            step(nc.vector.tensor_tensor(total[:, :], cum[:, :], bank[7][:, 0:ET], ALU.subtract))
            step(nc.vector.tensor_tensor(cnt_f[:, :], et(cum[:, :])[:, :, TILES - 1], et(total[:, :])[:, :, 0], ALU.subtract))
            step(nc.vector.tensor_scalar(cnt_i[:, :], cnt_f[:, :], float(SLOTS - 1), None, ALU.add))
            step(nc.vector.tensor_scalar(tiles_i[:, :], cnt_i[:, :], SLOTS.bit_length() - 1, None, ALU.arith_shift_right))
            step(nc.vector.tensor_copy(tiles_f[:, :], tiles_i[:, :]))
            step(nc.vector.tensor_tensor_scan(tile_end[:, :], ones_et[:, 0:E], tiles_f[:, :], 0.0, ALU.mult, ALU.add))
            step(nc.vector.tensor_tensor(run_off[:, :], tile_end[:, :], tiles_f[:, :], ALU.subtract))
            step(nc.vector.scalar_tensor_tensor(run_off[:, :], run_off[:, :], float(SLOTS), et(total[:, :])[:, :, 0],
                                                ALU.mult, ALU.subtract))
            step(nc.vector.tensor_tensor(ended[:, :].rearrange("p (j e) -> p j e", e=E),
                                         tile_end[:, :].unsqueeze(1).to_broadcast([P, EXPERT_TILES, E]),
                                         tile_no.rearrange("p (j e) -> p j e", e=E), ALU.is_le))
            step(nc.vector.tensor_reduce(owner_f[:, :], ended[:, :].rearrange("p (j e) -> p j e", e=E), AX.X, ALU.add))
            nc.vector.tensor_scalar(owner[:, :], owner_f[:, :], float(E - 1), None, ALU.min).then_inc(r_owner, 1)
            step(nc.vector.tensor_tensor(pos[:, :], total[:, :], bank[6][:, 0:ET], ALU.add))
            step(nc.vector.tensor_tensor(et(pos[:, :]), et(pos[:, :]), over_t(run_off[:, :]), ALU.add))
            nc.vector.tensor_tensor(picked[:, 0, :], choice[:, 0, :], pos[:, :], ALU.mult).then_inc(r_step, 1)
            steps[0] += 1
            step(nc.vector.tensor_tensor(picked[:, 1, :], choice[:, 1, :], pos[:, :], ALU.mult))
            nc.vector.tensor_reduce(slot_f[:, 0, :], te(picked[:, 0, :]), AX.X, ALU.add).then_inc(r_step, 1)
            steps[0] += 1
            step(nc.vector.tensor_reduce(slot_f[:, 1, :], te(picked[:, 1, :]), AX.X, ALU.add))
            slots = slot_f[:, :, :].rearrange("p k t -> p (k t)")
            step(nc.vector.tensor_copy(slot_i[:, :], slots))
            nc.vector.tensor_scalar(low_i[:, :], slot_i[:, :], P - 1, None, ALU.bitwise_and).then_inc(r_step, 1)
            step(nc.vector.tensor_scalar(high_i[:, :], slot_i[:, :], P.bit_length() - 1, None, ALU.arith_shift_right))
            steps[0] += 1
            dve.wait_ge(r_step, steps[0])
            nc.vector.tensor_copy(low16[:, :], low_i[:, :]).then_inc(r_split, 1)
            nc.vector.tensor_copy(high[:, :], high_i[:, :]).then_inc(r_split, 1)
            nc.vector.tensor_copy(slot[:, :, :], slot_f[:, :, :]).then_inc(r_slot, 1)

            dve.wait_ge(r_split, 2)
            dve.wait_ge(a_lo, BATCH)
            with dve.Fori(0, INV_STEPS // INV_RING) as i:
                for u in range(INV_RING):
                    q = INV_RING * i + u
                    dve.wait_ge(i_mm, q + 1)
                    nc.vector.tensor_copy(high_st[:, u, :], high[:, ds(q * CHUNK, CHUNK)]).then_inc(i_st, 1)
                    nc.vector.tensor_copy(token_st[:, u, :], token[:, ds(q * CHUNK, CHUNK)]).then_inc(i_st, 1)
                    nc.vector.tensor_tensor(low_hot[:, u, :, :], iota16[:, :].unsqueeze(1).to_broadcast([P, CHUNK, P]),
                                            low16[:, ds(q * CHUNK, CHUNK)].unsqueeze(2).to_broadcast([P, CHUNK, P]),
                                            ALU.is_equal)
                    dve.wait_ge(i_st, 2 * q + 2)
                    for c in range(POOL_ROWS, CHUNK):
                        last = nc.vector.tensor_scalar(high_token[:, u, c, :], iota16[:, 0:SUBTILES], high_st[:, u, c:c + 1],
                                                       token_st[:, u, c:c + 1], ALU.is_equal, ALU.mult)
                    last.then_inc(i_high, 1)
            dve.wait_ge(i_mm, INV_STEPS + INV_RING)
            nc.vector.tensor_scalar(slot_token[:, :], bank[4][:, 0:SUBTILES], float(TOKENS // 2), None, ALU.add).then_inc(i_map, 1)

            def weight_low(t, c):
                j, k, use, _ = t
                if c == 0:
                    dve.wait_ge(e_w1[k], 16 * use + 16)
                    nc.vector.tensor_copy(eb1[:, k % 2, :], e1_sb[k][:, 2 * HR:W1_ALL])
                dve.wait_ge(e_whi, CR * j + c + 1)
                at = slice(c * 2 * P, (c + 1) * 2 * P)
                nc.vector.tensor_tensor(e1_lo[:, k % 2, at], e1_sb[k][:, at], e1_hi[:, k % 2, at].bitcast(fp32),
                                        ALU.subtract).then_inc(e_wlo, 1)

            def rows_low(t):
                j, u = t[0], t[1] % 2
                dve.wait_ge(e_xhi, j + 1 + RING)
                nc.vector.tensor_tensor(xsT_lo[:, u, :], bank[2 + u][:, 0:SLOTS], xsT_hi[:, u, :].bitcast(fp32),
                                        ALU.subtract).then_inc(e_xlo, 1)

            def expert_act(t, after):
                j, u = t[0], t[1] % 2
                for c in range(CR):
                    m = CR * j + c
                    g = (CR * u + c) % 2
                    dve.wait_ge(e_a, m + 1)
                    dve.wait_ge(e_gate, m + 1 + RING)
                    nc.vector.scalar_tensor_tensor(eact[:, u, c, :], bank[6 + g][:, 0:SLOTS], eb1[:, u, c:c + 1],
                                                   egate[:, g, :], ALU.add, ALU.mult).then_inc(e_act, 1)
                    if after:
                        if c == 0:
                            dve.wait_ge(e_act, CR * j + RING)
                        if c == 1:
                            rows_low(after)
                        weight_low(after, c)

            def expert_rows(t):
                j, k, _, pair = t
                u = k % 2
                dve.wait_ge(e_y, j + 1 + RING)
                dve.wait_ge(e_st[u], 16 * pair + 16)
                for s in range(SUB):
                    last = nc.vector.tensor_tensor(ys_sb[:, u, s, :], bank[u][:, s * D:(s + 1) * D], e2_sb[k][:, CR * D:W2_ALL], ALU.add)
                last.then_inc(e_yev, 1)

            for c in range(CR):
                weight_low(expert_tile(0, 0), c)
            rows_low(expert_tile(0, 0))
            expert_act(expert_tile(0, 0), expert_tile(0, 1))
            with dve.Fori(0, E_TURNS) as i:
                for n in range(1, 1 + WEIGHT_RING):
                    expert_act(expert_tile(i, n), expert_tile(i, n + 1))
                    expert_rows(expert_tile(i, n - 1))
            for n in range(1 + WEIGHT_RING * E_TURNS, EXPERT_TILES):
                expert_act(expert_tile(0, n), expert_tile(0, n + 1) if n + 1 < EXPERT_TILES else None)
                expert_rows(expert_tile(0, n - 1))
            expert_rows(expert_tile(0, EXPERT_TILES - 1))

            def scores_out(i, k):
                u, j = k // TPB, k % TPB
                w = SEQ - j * P
                dve.wait_ge(c_s, 2 * TPB * i + k + 1)
                nc.vector.tensor_tensor(sT[:, u, j, 0:w], bank[SCORE_BANKS[k % 4]][:, 0:w], mask[:, 0:w], ALU.mult).then_inc(c_mask, 1)

            def row_stats(b, u):
                dve.wait_ge(c_o, b + 1 + RING)
                for t in range(TPB):
                    last = nc.vector.bn_stats(o_stats[:, u * TPB + t, :], bank[u][:, t * D:(t + 1) * D])
                last.then_inc(c_stat, 1)

            def shared_act(i, k):
                m = 2 * CS * i + k
                c = k % CS
                dve.wait_ge(d_a, m + 1)
                dve.wait_ge(d_gate, m + 1 + RING)
                if c == 0:
                    dve.wait_ge(d_y, 2 * i + k // CS + 1)
                nc.vector.scalar_tensor_tensor(act_sb[:, k // CS, c, :], bank[6 + k % 2][:, :], bcol[:, B_S1 + c:B_S1 + c + 1],
                                               gate_sb[:, k % 2, :], ALU.add, ALU.mult).then_inc(d_act, 1)

            def add_attention(b):
                at = ds(b * TPB, TPB)
                dve.wait_ge(c_on, b + 1 + RING)
                nc.vector.tensor_tensor(on_all[:, at, :], on_all[:, at, :],
                                        brow[:, R_LNW:R_LNW + D].unsqueeze(1).to_broadcast([P, TPB, D]), ALU.mult).then_inc(f_w, 1)
                dve.wait_ge(f_w, b + 1)
                dve.wait_ge(f_y1, b + 1)
                dve.wait_ge(d_acc, b + 1 + RING)
                nc.vector.tensor_tensor(acc[:, at, :], acc[:, at, :], on_all[:, at, :], ALU.add).then_inc(f_res, 1)

            def add_shared(b, u, after_experts=False):
                at = ds(b * TPB, TPB)
                dve.wait_ge(d_y, b + 1 + RING)
                if u == 0 or after_experts:
                    dve.wait_ge(f_y1, b + 1)
                nc.vector.tensor_tensor(acc[:, at, :], acc[:, at, :], bank[2 + u][:, :].rearrange("p (t d) -> p t d", d=D),
                                        ALU.add).then_inc(d_acc, 1)

            def add_experts(b, u, k, before_shared=False):
                at = ds(b * TPB, TPB)
                dve.wait_ge(f_scaled, TOP * b + k + 1)
                if k == 1:
                    dve.wait_ge(f_y0, b + 1)
                elif u == 1 and not before_shared:
                    dve.wait_ge(d_acc, b + 1 + RING)
                nc.vector.tensor_tensor(acc[:, at, :], acc[:, at, :], y_st[:, u, k, :, :], ALU.add).then_inc((f_y0, f_y1)[k], 1)

            def root(i, n):
                if n == 0:
                    dve.wait_ge(c_var, i + 1)
                else:
                    dve.wait_ge(c_root, ROOT_STEPS * i + n)
                y, v, prod = o_rstd[:, :], o_var_eps[:, :], o_prod[:, :]
                if n == 0:
                    ins = nc.vector.tensor_scalar(o_bits[:, :], v.bitcast(i32), 1, None, ALU.arith_shift_right)
                elif n == 1:
                    ins = nc.vector.tensor_scalar(y.bitcast(i32), o_bits[:, :], -1.0, float(0x5f3759df), ALU.mult, ALU.add)
                elif n % 3 == 2:
                    ins = nc.vector.tensor_tensor(prod, y, v, ALU.mult)
                elif n % 3 == 0:
                    ins = nc.vector.scalar_tensor_tensor(prod, y, -0.5, prod, ALU.mult, ALU.mult)
                else:
                    ins = nc.vector.scalar_tensor_tensor(y, prod, 1.5, y, ALU.add, ALU.mult)
                ins.then_inc(c_root, 1)

            def choice_weights():
                dve.wait_ge(r_exp, 1)
                step(nc.vector.tensor_scalar(denom[:, :], ratio[:, :], 1.0, None, ALU.add))
                step(nc.vector.reciprocal(weight[:, 0, :], denom[:, :]))
                nc.vector.tensor_tensor(weight[:, 1, :], ratio[:, :], weight[:, 0, :], ALU.mult).then_inc(f_weight, 1)

            def tail_turn(i, first, last=False):
                for k in range(2 * TPB):
                    scores_out(i, k)
                if first:
                    choice_weights()
                else:
                    for k in range(TOP):
                        add_experts(2 * i - 1, 1, k)
                    add_attention(2 * i - 2)
                    add_attention(2 * i - 1)
                row_stats(2 * i, 0)
                row_stats(2 * i + 1, 1)
                dve.wait_ge(c_stat, 2 * i + 2)
                moments(o_stats[:, :, :], o_mean[:, :], o_var_eps[:, :], o_diff[:, :], c_step, 6 * i, c_var)
                shared_act(i, 0)
                root(i, 0)
                root(i, 1)
                shared_act(i, 1)
                root(i, 2)
                root(i, 3)
                shared_act(i, 2)
                root(i, 4)
                root(i, 5)
                add_experts(2 * i, 0, 0)
                root(i, 6)
                root(i, 7)
                shared_act(i, 3)
                root(i, 8)
                root(i, 9)
                add_experts(2 * i, 0, 1)
                root(i, 10)
                dve.wait_ge(c_root, ROOT_STEPS * (i + 1))
                nc.vector.scalar_tensor_tensor(o_shift[:, :], o_mean[:, :], -1.0, o_rstd[:, :], ALU.mult, ALU.mult).then_inc(c_shift, 1)
                add_shared(2 * i, 0)
                if last:
                    for k in range(TOP):
                        add_experts(BATCH - 1, 1, k, True)
                add_shared(2 * i + 1, 1, last)

            dve.wait_ge(e_side, 2 * SIDE_PAIRS)
            tail_turn(0, True)
            with dve.Fori(1, PAIRS - 1) as i:
                tail_turn(i, False)
            tail_turn(PAIRS - 1, False, True)
            add_attention(BATCH - 2)
            add_attention(BATCH - 1)

        @block.tensor
        def _(pe):
            mm = nc.tensor.matmul
            for s in (b_o, e_tr, e_y, c_o, d_y):
                pe.sem_inc(s, RING)
            pe.sem_inc(i_mm, INV_RING)

            def split_mm(dst, w_high, w_low, x_high, x_low):
                mm(dst, w_high, x_high, start=True, stop=False)
                mm(dst, w_high, x_low, start=False, stop=False)
                return mm(dst, w_low, x_high, start=False, stop=True)

            def keep_warm():
                for _ in range(KEEP_WARM):
                    mm(bank[7][:, 0:P], zeros16[:, :], zeros16[:, :], start=True, stop=True)

            pe.wait_ge(set_up, 3)
            pe.wait_ge(x_in[1], 16)
            with pe.Fori(0, WARM // 8) as i:
                for _ in range(8):
                    mm(bank[7][:, 0:P], zeros16[:, :], zeros16[:, :], start=True, stop=True)
            pe.wait_ge(ident_in, 32)
            def logits(b):
                pe.wait_ge(a_st, b + 1)
                for t in range(TPB):
                    last = mm(bank[6][:, (b * TPB + t) * E:(b * TPB + t + 1) * E], xnT[b][:, t * P:(t + 1) * P], wr_sb[:, :],
                              start=True, stop=True)
                last.then_inc(a_lg, 1)

            for b in range(BATCH):
                pe.wait_ge(a_xn, b + 1)
                pe.wait_ge(a_xn_act, b + 1)
                if b >= 2:
                    pe.wait_ge(a_hi, b - 1)
                for t in range(TPB):
                    last = nc.tensor.transpose(bank[4 + b % 2][:, t * P:(t + 1) * P], xn_all[:, b * TPB + t, :], ident)
                last.then_inc(a_tr, 1)
                keep_warm()
                if b:
                    logits(b - 1)
            logits(BATCH - 1)

            def hidden(m):
                b, n = m // 3, m % 3
                if m:
                    pe.wait_ge(b_gelu, m)
                if m == 2:
                    pe.wait_ge(a_hi, BATCH)
                if n == 0:
                    pe.wait_ge(a_lo, b + 1)
                split_mm(bank[HIDDEN_BANKS[n]][:, :], w1_hi[:, n * D:(n + 1) * D], w1_lo[:, n * D:(n + 1) * D],
                         xT_hi[:, ds(b * SEQ, SEQ)], xT_lo[:, ds(b * SEQ, SEQ)]).then_inc(b_h, 1)

            def second(m):
                n, h = m % 3, m % 2
                pe.wait_ge(b_gelu, m + 1 + RING)
                pe.wait_ge(b_evac, m + 1)
                if n < 2:
                    mm(bank[2 + h][:, :], w2_sb[:, n, :], h_sb[:, h, :], start=True, stop=True).then_inc(b_o, 1)
                else:
                    for t in range(TPB):
                        last = mm(bank[2 + h][:, t * D:(t + 1) * D], h_sb[:, h, t * P:(t + 1) * P], w2_sb[:, n, :],
                                  start=True, stop=True)
                    last.then_inc(b_o, 1)

            def ranks():
                pe.wait_ge(r_taken, 1)
                pe.wait_ge(cast, 2)
                pe.wait_ge(set_up, 4)
                mm(bank[6][:, 0:ET], before16[:, :], taken[:, :], start=True, stop=True).then_inc(r_rank, 1)
                mm(bank[7][:, 0:ET], ones16[:, :], taken[:, :], start=True, stop=True).then_inc(r_rank, 1)

            def invert(q):
                pe.wait_ge(i_high, q + 1)
                pe.wait_ge(i_pool, q + 1)
                for c in range(CHUNK):
                    last = mm(bank[4][:, 0:SUBTILES], low_hot[:, q % INV_RING, c, :], high_token[:, q % INV_RING, c, :],
                              start=(q == 0 and c == 0), stop=(q == INV_STEPS - 1 and c == CHUNK - 1))
                last.then_inc(i_mm, 1)

            pe.wait_ge(w_low, 1)
            RANKS_AFTER = 3
            INVERT_AFTER = [12, 13, 14, 16, 17, 18, 19, 20]
            hidden(0)
            hidden(1)
            for i in range(PAIRS):
                for k in range(6):
                    if 6 * i + k + 2 < B_ITEMS:
                        hidden(6 * i + k + 2)
                    second(6 * i + k)
                    if 6 * i + k == RANKS_AFTER:
                        ranks()
                    if 6 * i + k in INVERT_AFTER:
                        invert(INVERT_AFTER.index(6 * i + k))

            def slot_transposes(t):
                j, k, _, pair = t
                u = k % 2
                pe.wait_ge(e_x[u], 16 * SUB * pair + 16 * SUB)
                pe.wait_ge(e_xlo, j + 1)
                for s in range(SUB):
                    last = nc.tensor.transpose(bank[2 + u][:, s * P:(s + 1) * P], xs_sb[:, u, s, :], ident)
                last.then_inc(e_tr, 1)

            def expert_up(t, c):
                j, u = t[0], t[1] % 2
                m = CR * j + c
                g = (CR * u + c) % 2
                if c == 0:
                    pe.wait_ge(e_xlo, j + 1 + RING)
                pe.wait_ge(e_wlo, m + 1 + RING * CR)
                pe.wait_ge(e_gate, m + 1)
                at = slice((2 * c + 1) * P, (2 * c + 2) * P)
                split_mm(bank[4 + g][:, 0:SLOTS], e1_hi[:, u, at], e1_lo[:, u, at], xsT_hi[:, u, :], xsT_lo[:, u, :]).then_inc(e_g, 1)
                pe.wait_ge(e_act, m + 1)
                at = slice(2 * c * P, (2 * c + 1) * P)
                split_mm(bank[6 + g][:, 0:SLOTS], e1_hi[:, u, at], e1_lo[:, u, at], xsT_hi[:, u, :], xsT_lo[:, u, :]).then_inc(e_a, 1)

            def expert_down(t, c):
                j, k, use, _ = t
                u = k % 2
                if c == 0:
                    pe.wait_ge(e_w2[k], 16 * use + 16)
                    pe.wait_ge(e_yev, j + 1)
                pe.wait_ge(e_act, CR * j + c + 1 + RING)
                for s in range(SUB):
                    last = mm(bank[u][:, s * D:(s + 1) * D], eact[:, u, c, s * P:(s + 1) * P], e2_sb[k][:, c * D:(c + 1) * D],
                              start=(c == 0 and s == 0), stop=(c == CR - 1 and s == SUB - 1))
                if c == CR - 1:
                    last.then_inc(e_y, 1)

            def expert(t, before, after):
                for c in range(CR):
                    expert_up(t, c)
                    if c == 1 and after:
                        slot_transposes(after)
                    if before:
                        expert_down(before, c)

            pe.wait_ge(w_low, 2)
            pe.wait_ge(b_evac, B_ITEMS + RING)
            pe.wait_ge(i_map, 1)
            keep_warm()
            slot_transposes(expert_tile(0, 0))
            keep_warm()
            expert(expert_tile(0, 0), None, expert_tile(0, 1))
            with pe.Fori(0, E_TURNS) as i:
                for n in range(1, 1 + WEIGHT_RING):
                    expert(expert_tile(i, n), expert_tile(i, n - 1), expert_tile(i, n + 1))
            for n in range(1 + WEIGHT_RING * E_TURNS, EXPERT_TILES):
                expert(expert_tile(0, n), expert_tile(0, n - 1), expert_tile(0, n + 1) if n + 1 < EXPERT_TILES else None)
            for c in range(CR):
                expert_down(expert_tile(0, EXPERT_TILES - 1), c)

            def scores(i, k):
                u, j = k // TPB, k % TPB
                b = 2 * i + u
                if j == 0:
                    pe.wait_ge(c_k, b + 1)
                if k < 2:
                    pe.wait_ge(d_acc, 2 * i + k + 1)
                elif k < 4:
                    pe.wait_ge(d_act, 2 * CS * i + RING)
                else:
                    pe.wait_ge(c_mask, 2 * TPB * i + k - 3 + RING)
                mm(bank[SCORE_BANKS[k % 4]][:, 0:SEQ - j * P], kT_st[:, u, j * P:(j + 1) * P],
                   qT_all[:, ds(b * SEQ + j * P, SEQ - j * P)], start=True, stop=True).then_inc(c_s, 1)

            def attend(i, u):
                b = 2 * i + u
                pe.wait_ge(c_mask, 2 * TPB * i + TPB * (u + 1) + RING)
                pe.wait_ge(e_yev, EXPERT_TILES + RING)
                pe.wait_ge(c_on, b + 1)
                for t in range(TPB):
                    for j in range(t + 1):
                        last = mm(bank[u][:, t * D:(t + 1) * D], sT[:, u, j, (t - j) * P:(t - j + 1) * P],
                                  v_all[:, ds(b * TPB + j, 1), :].rearrange("p a d -> p (a d)"), start=(j == 0), stop=(j == t))
                last.then_inc(c_o, 1)

            def shared_up(i, k):
                m = 2 * CS * i + k
                c = k % CS
                at = ds((2 * i + k // CS) * SEQ, SEQ)
                pe.wait_ge(d_gate, m + 1)
                cols = slice(HS + c * P, HS + (c + 1) * P)
                split_mm(bank[4 + k % 2][:, :], ws1_hi[:, cols], ws1_lo[:, cols], xT_hi[:, at], xT_lo[:, at]).then_inc(d_g, 1)
                pe.wait_ge(d_act, m + 1)
                cols = slice(c * P, (c + 1) * P)
                split_mm(bank[6 + k % 2][:, :], ws1_hi[:, cols], ws1_lo[:, cols], xT_hi[:, at], xT_lo[:, at]).then_inc(d_a, 1)

            def shared_down(i, u):
                pe.wait_ge(d_act, 2 * CS * i + CS * (u + 1) + RING)
                pe.wait_ge(c_mask, 2 * TPB * (i + 1) + RING)
                for t in range(TPB):
                    for c in range(CS):
                        last = mm(bank[2 + u][:, t * D:(t + 1) * D], act_sb[:, u, c, t * P:(t + 1) * P], ws2_sb[:, c, :],
                                  start=(c == 0), stop=(c == CS - 1))
                last.then_inc(d_y, 1)

            pe.wait_ge(e_side, 2 * SIDE_PAIRS)
            with pe.Fori(0, PAIRS) as i:
                for k in range(2 * TPB):
                    scores(i, k)
                attend(i, 0)
                attend(i, 1)
                for k in range(2 * CS):
                    shared_up(i, k)
                shared_down(i, 0)
                shared_down(i, 1)


def kernel(**inputs):
    import numpy as np
    import concourse.bacc as bacc
    from concourse.bass_utils import run_bass_kernel_spmd

    def a(name):
        return np.ascontiguousarray(inputs["L0_" + name])

    c = np.zeros((P, C_ALL), np.float32)
    row, col = np.arange(P)[:, None], np.arange(P)[None, :]
    c[:, C_ID:C_ID + P] = row == col
    c[:, C_MASK:C_MASK + SEQ] = 1.0
    c[:, C_MASK:C_MASK + P] = col >= row
    c[:, C_BEFORE:C_BEFORE + P] = row < col
    c[:, C_REV:C_REV + ET] = np.repeat(E - np.arange(E), TILES)
    c[:, C_TILE:C_IOTA] = np.repeat(np.arange(EXPERT_TILES), E)
    c[:, C_IOTA:C_TOKEN] = col
    c[:, C_TOKEN:C_ALL] = np.tile(np.arange(TILES), TOP)[None, :] * P + row - TOKENS // 2
    cols = [a(f"attn_b1{n}") for n in "qkv"] + [a("attn_b2q"), a("attn_b2k")]
    cols = np.concatenate([np.stack(cols), a("ffn_bs1").reshape(-1, P)])
    rows = np.concatenate([a("ffn_br"), a("attn_b2v"), a("attn_ln_w"), a("attn_ln_b"), a("ffn_bs2")])
    we1 = a("ffn_We1").reshape(E, P, 2, CR, P).transpose(0, 1, 3, 2, 4).reshape(E, P, 2 * HR)
    be1 = a("ffn_be1").reshape(E, 2 * CR, P).transpose(0, 2, 1)
    we2 = a("ffn_We2").reshape(E, CR, P, D).transpose(0, 2, 1, 3).reshape(E, P, CR * D)
    be2 = np.broadcast_to(a("ffn_be2")[:, None, :], (E, P, D))
    arrays = {
        "x": a("attn_x"), "w1": np.stack([a(f"attn_W1{n}") for n in "qkv"]), "w2": np.stack([a(f"attn_W2{n}") for n in "qkv"]),
        "ws1": a("ffn_Ws1"), "ws2": a("ffn_Ws2"), "expert1": np.concatenate([we1, be1], axis=2),
        "expert2": np.concatenate([we2, be2], axis=2), "wr": a("ffn_Wr"), "consts": c,
        "bias_cols": np.ascontiguousarray(cols.T), "bias_rows": np.ascontiguousarray(np.broadcast_to(rows[None, :], (P, rows.size))),
    }
    nc = bacc.Bacc("TRN2", target_bir_lowering=False, num_devices=1)
    args = [nc.dram_tensor(f"in_{n}", v.shape, mybir.dt.from_np(v.dtype), kind="ExternalInput").ap() for n, v in arrays.items()]
    out = nc.dram_tensor("out_0", (BATCH, SEQ, D), mybir.dt.float32, kind="ExternalOutput").ap()
    block_kernel(nc, *args, out)
    r = run_bass_kernel_spmd(nc, [{f"in_{n}": v for n, v in arrays.items()}], core_ids=[0])
    return r.results[0]["out_0"]
```
